# Optimizing a Trainium2 kernel written in Bass

```python
import numpy as np
import jax
import jax.numpy as jnp

def _softmax(x, axis=-1):
    return jax.nn.softmax(x, axis=axis)

def _gelu(x):
    return jax.nn.gelu(x, approximate=True)

def _silu(x):
    return jax.nn.silu(x)

def _sigmoid(x):
    return jax.nn.sigmoid(x)

def _layernorm(x, axis=-1, eps=1e-05):
    m = jnp.mean(x, axis=axis, keepdims=True)
    v = jnp.var(x, axis=axis, keepdims=True)
    return (x - m) / jnp.sqrt(v + eps)

def _scatter_add(tgt, idx, src, axis=0):
    return tgt.at[idx].add(src)

def _segment_sum(src, seg, n):
    return jax.ops.segment_sum(src, seg, n)
kernel_name = 'mk_adaln_ffn_d2_seqx_r8_ef1dfe'

def setup_inputs(seed: int=0):
    np.random.seed(seed)
    _w = jnp.asarray

    def _rec_inputs():
        import jax
        import jax.numpy as jnp
        _rk = jax.random.key(seed)
        x = -0.0003929 + 0.9999 * jax.random.normal(jax.random.fold_in(_rk, 1), (8, 256, 128), jnp.float32)
        _lenS = 256 - jax.random.randint(jax.random.fold_in(_rk, 7), (8,), 0, max(1, 256 // 4) + 1, jnp.int32)
        _lenS2 = 256 - jax.random.randint(jax.random.fold_in(_rk, 8), (8,), 0, max(1, 256 // 4) + 1, jnp.int32)
        itok_B_0_7 = jax.random.randint(jax.random.fold_in(_rk, 11), (8,), 0, 8, jnp.int32)
        itok_B_0_3 = jax.random.randint(jax.random.fold_in(_rk, 12), (8,), 0, 4, jnp.int32)
        return (x, itok_B_0_7, itok_B_0_3)
    x, itok_B_0_7, itok_B_0_3 = _rec_inputs()

    def _L0_cond_setup():
        import jax, jax.numpy as jnp
        import numpy as np
        B, S, D, F = (32, 64, 128, 512)
        R_COMMON, R_DOMAIN, E = (16, 16, 8)
        ALPHA = 2.0

        def _expert_lora(x, expert_ids, Wa, Wb):
            Ab = Wa[expert_ids]
            Bb = Wb[expert_ids]
            low = jnp.einsum('bsd,brd->bsr', x, Ab)
            return ALPHA * jnp.einsum('bsr,bor->bso', low, Bb)
        key = jax.random.key(seed)
        ks = jax.random.split(key, 12)
        sd = lambda k, shape: jax.random.normal(k, shape, dtype=jnp.float32) * (1.0 / np.sqrt(shape[-1]))
        return {'hidden_states': jax.random.normal(ks[0], (B, S, D), dtype=jnp.float32), 'expert_ids': jax.random.randint(ks[1], (B,), 0, E, dtype=jnp.int32), 'wi': sd(ks[2], (F, D)), 'wo': sd(ks[3], (D, F)), 'common_wi_a': sd(ks[4], (R_COMMON, D)), 'common_wi_b': sd(ks[5], (F, R_COMMON)), 'common_wo_a': sd(ks[6], (R_COMMON, F)), 'common_wo_b': sd(ks[7], (D, R_COMMON)), 'experts_wi_a': sd(ks[8], (E, R_DOMAIN, D)), 'experts_wi_b': sd(ks[9], (F, R_DOMAIN)) * jnp.ones((E, 1, 1)) * 0.0 + sd(ks[9], (E, F, R_DOMAIN)), 'experts_wo_a': sd(ks[10], (E, R_DOMAIN, F)), 'experts_wo_b': sd(ks[11], (E, D, R_DOMAIN))}
    _L0_cond_all = _L0_cond_setup()
    _L0_cond_in = {k: v for k, v in _L0_cond_all.items() if k in ('wi', 'wo', 'common_wi_a', 'common_wi_b', 'common_wo_a', 'common_wo_b', 'experts_wi_a', 'experts_wi_b', 'experts_wo_a', 'experts_wo_b')}
    del _L0_cond_all

    def _L0_ffn_setup():
        import jax, jax.numpy as jnp
        import numpy as np
        B, S, H, F, E, R, TOPK = (4, 256, 128, 512, 4, 4, 2)

        def _more_forward(x, Wg, bg, W1, b1, W2, b2):
            b, s, h = x.shape
            cur = x
            for r in range(R):
                flat = cur.reshape(-1, h)
                logits = flat @ Wg[r] + bg[r]
                vals, idx = jax.lax.top_k(logits, TOPK)
                w = jax.nn.softmax(vals, axis=-1)
                cw = jnp.sum(jax.nn.one_hot(idx, E, dtype=flat.dtype) * w[..., None], axis=1)
                hmid = jax.nn.gelu(jnp.einsum('nh,ehf->enf', flat, W1) + b1[:, None, :])
                y = jnp.einsum('enf,efh->enh', hmid, W2) + b2[:, None, :]
                out = jnp.einsum('ne,enh->nh', cw, y)
                cur = cur + out.reshape(b, s, h)
            return cur
        key = jax.random.key(seed)
        ks = jax.random.split(key, 8)
        scale = 0.02
        return {'x': jax.random.normal(ks[0], (B, S, H), dtype=jnp.float32), 'Wg': jax.random.normal(ks[1], (R, H, E), dtype=jnp.float32) * scale, 'bg': jnp.zeros((R, E), dtype=jnp.float32), 'W1': jax.random.normal(ks[2], (E, H, F), dtype=jnp.float32) * scale, 'b1': jnp.zeros((E, F), dtype=jnp.float32), 'W2': jax.random.normal(ks[3], (E, F, H), dtype=jnp.float32) * scale, 'b2': jnp.zeros((E, H), dtype=jnp.float32)}
    _L0_ffn_all = _L0_ffn_setup()
    _L0_ffn_in = {k: v for k, v in _L0_ffn_all.items() if k in ('Wg', 'bg', 'W1', 'b1', 'W2', 'b2')}
    del _L0_ffn_all

    def _L1_cond_setup():
        import jax, jax.numpy as jnp
        import numpy as np
        D = 128
        RANK = 16
        ALPHA = 16.0
        SCALING = ALPHA / RANK
        N_LANG = 4
        B, S = (32, 256)
        key = jax.random.key(seed)
        k1, k2, k3, k4, k5 = jax.random.split(key, 5)
        x = jax.random.normal(k1, (B, S, D), dtype=jnp.float32)
        language_ids = jax.random.randint(k2, (B,), 0, N_LANG, dtype=jnp.int32)
        lora_A = jax.random.normal(k3, (N_LANG, RANK, D), dtype=jnp.float32) * 0.02
        lora_B = jax.random.normal(k4, (N_LANG, D, RANK), dtype=jnp.float32) * 0.02
        lang_embed = jax.random.normal(k5, (N_LANG, D), dtype=jnp.float32) * 0.02
        return {'x': x, 'language_ids': language_ids, 'lora_A': lora_A, 'lora_B': lora_B, 'lang_embed': lang_embed}
    _L1_cond_all = _L1_cond_setup()
    _L1_cond_in = {k: v for k, v in _L1_cond_all.items() if k in ('lora_A', 'lora_B', 'lang_embed')}
    del _L1_cond_all

    def _L1_ffn_setup():
        import jax, jax.numpy as jnp
        import numpy as np
        D_IN, D_HID = (128, 512)

        def _ternary(key, shape):
            return jax.random.randint(key, shape, -1, 2).astype(jnp.float32)

        def _tlin(x, w, s):
            return jnp.einsum('bsi,oi->bso', x, w) * s
        key = jax.random.key(seed)
        ks = jax.random.split(key, 12)
        inv = lambda fan: 1.0 / np.sqrt(fan).astype(np.float32)
        return {'x': jax.random.normal(ks[0], (4, 256, D_IN), dtype=jnp.float32), 'w1_w': _ternary(ks[1], (D_HID, D_IN)), 'w1_s': jax.random.uniform(ks[2], (D_HID,), dtype=jnp.float32) * inv(D_IN), 'w2_w': _ternary(ks[3], (D_HID, D_IN)), 'w2_s': jax.random.uniform(ks[4], (D_HID,), dtype=jnp.float32) * inv(D_IN), 'h1_w': _ternary(ks[5], (D_HID, D_HID)), 'h1_s': jax.random.uniform(ks[6], (D_HID,), dtype=jnp.float32) * inv(D_HID), 'h2_w': _ternary(ks[7], (D_HID, D_HID)), 'h2_s': jax.random.uniform(ks[8], (D_HID,), dtype=jnp.float32) * inv(D_HID), 'w3_w': _ternary(ks[9], (D_IN, D_HID)), 'w3_s': jax.random.uniform(ks[10], (D_IN,), dtype=jnp.float32) * inv(D_HID)}
    _L1_ffn_all = _L1_ffn_setup()
    _L1_ffn_in = {k: v for k, v in _L1_ffn_all.items() if k in ('w1_w', 'w1_s', 'w2_w', 'w2_s', 'h1_w', 'h1_s', 'h2_w', 'h2_s', 'w3_w', 'w3_s')}
    del _L1_ffn_all
    return {'x': x, 'itok_B_0_7': itok_B_0_7, 'itok_B_0_3': itok_B_0_3, 'L0_cond_wi': _L0_cond_in['wi'], 'L0_cond_wo': _L0_cond_in['wo'], 'L0_cond_common_wi_a': _L0_cond_in['common_wi_a'], 'L0_cond_common_wi_b': _L0_cond_in['common_wi_b'], 'L0_cond_common_wo_a': _L0_cond_in['common_wo_a'], 'L0_cond_common_wo_b': _L0_cond_in['common_wo_b'], 'L0_cond_experts_wi_a': _L0_cond_in['experts_wi_a'], 'L0_cond_experts_wi_b': _L0_cond_in['experts_wi_b'], 'L0_cond_experts_wo_a': _L0_cond_in['experts_wo_a'], 'L0_cond_experts_wo_b': _L0_cond_in['experts_wo_b'], 'L0_ffn_Wg': _L0_ffn_in['Wg'], 'L0_ffn_bg': _L0_ffn_in['bg'], 'L0_ffn_W1': _L0_ffn_in['W1'], 'L0_ffn_b1': _L0_ffn_in['b1'], 'L0_ffn_W2': _L0_ffn_in['W2'], 'L0_ffn_b2': _L0_ffn_in['b2'], 'L1_cond_lora_A': _L1_cond_in['lora_A'], 'L1_cond_lora_B': _L1_cond_in['lora_B'], 'L1_cond_lang_embed': _L1_cond_in['lang_embed'], 'L1_ffn_w1_w': _L1_ffn_in['w1_w'], 'L1_ffn_w1_s': _L1_ffn_in['w1_s'], 'L1_ffn_w2_w': _L1_ffn_in['w2_w'], 'L1_ffn_w2_s': _L1_ffn_in['w2_s'], 'L1_ffn_h1_w': _L1_ffn_in['h1_w'], 'L1_ffn_h1_s': _L1_ffn_in['h1_s'], 'L1_ffn_h2_w': _L1_ffn_in['h2_w'], 'L1_ffn_h2_s': _L1_ffn_in['h2_s'], 'L1_ffn_w3_w': _L1_ffn_in['w3_w'], 'L1_ffn_w3_s': _L1_ffn_in['w3_s']}

def reference(x, itok_B_0_7, itok_B_0_3, L0_cond_wi, L0_cond_wo, L0_cond_common_wi_a, L0_cond_common_wi_b, L0_cond_common_wo_a, L0_cond_common_wo_b, L0_cond_experts_wi_a, L0_cond_experts_wi_b, L0_cond_experts_wo_a, L0_cond_experts_wo_b, L0_ffn_Wg, L0_ffn_bg, L0_ffn_W1, L0_ffn_b1, L0_ffn_W2, L0_ffn_b2, L1_cond_lora_A, L1_cond_lora_B, L1_cond_lang_embed, L1_ffn_w1_w, L1_ffn_w1_s, L1_ffn_w2_w, L1_ffn_w2_s, L1_ffn_h1_w, L1_ffn_h1_s, L1_ffn_h2_w, L1_ffn_h2_s, L1_ffn_w3_w, L1_ffn_w3_s):
    import jax
    import jax.numpy as jnp

    def _L0_cond_ref(hidden_states, expert_ids, wi, wo, common_wi_a, common_wi_b, common_wo_a, common_wo_b, experts_wi_a, experts_wi_b, experts_wo_a, experts_wo_b):
        import jax, jax.numpy as jnp
        import numpy as np
        B, S, D, F = (32, 64, 128, 512)
        R_COMMON, R_DOMAIN, E = (16, 16, 8)
        ALPHA = 2.0

        def _expert_lora(x, expert_ids, Wa, Wb):
            Ab = Wa[expert_ids]
            Bb = Wb[expert_ids]
            low = jnp.einsum('bsd,brd->bsr', x, Ab)
            return ALPHA * jnp.einsum('bsr,bor->bso', low, Bb)
        x = hidden_states
        hidden_i = jnp.einsum('bsd,fd->bsf', x, wi)
        hidden_i += ALPHA * jnp.einsum('bsr,fr->bsf', jnp.einsum('bsd,rd->bsr', x, common_wi_a), common_wi_b)
        hidden_i += _expert_lora(x, expert_ids, experts_wi_a, experts_wi_b)
        hidden_i = jax.nn.relu(hidden_i)
        hidden_o = jnp.einsum('bsf,df->bsd', hidden_i, wo)
        hidden_o += ALPHA * jnp.einsum('bsr,dr->bsd', jnp.einsum('bsf,rf->bsr', hidden_i, common_wo_a), common_wo_b)
        hidden_o += _expert_lora(hidden_i, expert_ids, experts_wo_a, experts_wo_b)
        return hidden_o

    def _L0_ffn_ref(x, Wg, bg, W1, b1, W2, b2):
        import jax, jax.numpy as jnp
        import numpy as np
        B, S, H, F, E, R, TOPK = (4, 256, 128, 512, 4, 4, 2)

        def _more_forward(x, Wg, bg, W1, b1, W2, b2):
            b, s, h = x.shape
            cur = x
            for r in range(R):
                flat = cur.reshape(-1, h)
                logits = flat @ Wg[r] + bg[r]
                vals, idx = jax.lax.top_k(logits, TOPK)
                w = jax.nn.softmax(vals, axis=-1)
                cw = jnp.sum(jax.nn.one_hot(idx, E, dtype=flat.dtype) * w[..., None], axis=1)
                hmid = jax.nn.gelu(jnp.einsum('nh,ehf->enf', flat, W1) + b1[:, None, :])
                y = jnp.einsum('enf,efh->enh', hmid, W2) + b2[:, None, :]
                out = jnp.einsum('ne,enh->nh', cw, y)
                cur = cur + out.reshape(b, s, h)
            return cur
        return _more_forward(x, Wg, bg, W1, b1, W2, b2)

    def _L1_cond_ref(x, language_ids, lora_A, lora_B, lang_embed):
        import jax, jax.numpy as jnp
        import numpy as np
        D = 128
        RANK = 16
        ALPHA = 16.0
        SCALING = ALPHA / RANK
        N_LANG = 4
        B, S = (32, 256)
        A = lora_A[language_ids]
        Bm = lora_B[language_ids]
        emb = lang_embed[language_ids]
        t = jnp.einsum('bsd,brd->bsr', x, A)
        lora_out = jnp.einsum('bsr,bdr->bsd', t, Bm) * SCALING
        return lora_out + emb[:, None, :]

    def _L1_ffn_ref(x, w1_w, w1_s, w2_w, w2_s, h1_w, h1_s, h2_w, h2_s, w3_w, w3_s):
        import jax, jax.numpy as jnp
        import numpy as np
        D_IN, D_HID = (128, 512)

        def _ternary(key, shape):
            return jax.random.randint(key, shape, -1, 2).astype(jnp.float32)

        def _tlin(x, w, s):
            return jnp.einsum('bsi,oi->bso', x, w) * s
        h = jax.nn.silu(_tlin(x, w1_w, w1_s)) * _tlin(x, w2_w, w2_s)
        h = jax.nn.gelu(_tlin(h, h1_w, h1_s), approximate=False)
        h = jax.nn.gelu(_tlin(h, h2_w, h2_s), approximate=False)
        return _tlin(h, w3_w, w3_s)
    x = x + _L0_ffn_ref(_L0_cond_ref(x, itok_B_0_7, L0_cond_wi, L0_cond_wo, L0_cond_common_wi_a, L0_cond_common_wi_b, L0_cond_common_wo_a, L0_cond_common_wo_b, L0_cond_experts_wi_a, L0_cond_experts_wi_b, L0_cond_experts_wo_a, L0_cond_experts_wo_b), L0_ffn_Wg, L0_ffn_bg, L0_ffn_W1, L0_ffn_b1, L0_ffn_W2, L0_ffn_b2)
    x = x + _L1_ffn_ref(_L1_cond_ref(x, itok_B_0_3, L1_cond_lora_A, L1_cond_lora_B, L1_cond_lang_embed), L1_ffn_w1_w, L1_ffn_w1_s, L1_ffn_w2_w, L1_ffn_w2_s, L1_ffn_h1_w, L1_ffn_h1_s, L1_ffn_h2_w, L1_ffn_h2_s, L1_ffn_w3_w, L1_ffn_w3_s)
    return x

_drawn_inputs = setup_inputs


def setup_inputs(seed=0):
    import zlib

    import numpy as np

    out = dict(_drawn_inputs(seed))
    spreads = {'L0_ffn_bg': (0.0, 0.1), 'L0_ffn_b1': (0.0, 0.1), 'L0_ffn_b2': (0.0, 0.1)}
    factors = {}
    for name, (base, spread) in spreads.items():
        noise = np.random.default_rng([zlib.crc32(name.encode()), seed]).standard_normal(out[name].shape)
        drawn = base * np.exp(spread * noise) if base else spread * noise
        out[name] = jnp.asarray(drawn.astype(out[name].dtype))
    for name, factor in factors.items():
        out[name] = (out[name] * factor).astype(out[name].dtype)
    return out
```

```python
from contextlib import ExitStack

import concourse.bass as bass
from concourse import mybir

ACT = mybir.ActivationFunctionType
ALU = mybir.AluOpType
AX_X = mybir.AxisListType.X
F32 = mybir.dt.float32
F32R = mybir.dt.float32r
I32 = mybir.dt.int32

P = 128
BATCHES, SEQ, D = 8, 256, 128
TOKENS = BATCHES * SEQ
CHUNK = 512
CHUNKS = TOKENS // CHUNK
PER_CHUNK = CHUNK // SEQ
F = 512
FC = F // P
RANK = 16
LORA_EXPERTS, LANGS = 8, 4
COND_ALPHA = 2.0
EXPERTS, ROUNDS = 4, 4
STEPS = CHUNKS * EXPERTS
BLOCKS = CHUNK // P
LORA_W = D + F + F + D
FFN_PIECES = 3 + 2 * FC
RING = 6
PAIRS = CHUNKS // 2

V_B1, V_B2, V_S1, V_S2, V_H1, V_H2, V_S3, V_WG = 0, 16, 20, 24, 28, 32, 36, 37
V_N = V_WG + ROUNDS * EXPERTS

MERGES = 2 * BATCHES + 2
Y_COND = BATCHES
Y_MOE = Y_COND + ROUNDS * STEPS
ADD0 = 2
ADD_MOE = ADD0 + ROUNDS * STEPS
LO_MOE = 2 * ROUNDS * STEPS
Z_ALL = 2 * CHUNKS
GATE_OPS = 11


def adaln_ffn(nc, x_t, ids0, ids1, cond_base, lora_common, lora_expert, lang_lora, lang_embed,
              moe_w, vecs, gate_bias, ffn_w, out_t):
    ctx = ExitStack()
    with ctx:
        def sb(name, shape, dt):
            return ctx.enter_context(nc.sbuf_tensor(name, shape, dt))

        def sem(name):
            return ctx.enter_context(nc.semaphore(name))

        x0 = sb("x0", [P, CHUNKS, CHUNK], F32)
        cur = sb("cur", [P, CHUNKS, CHUNK], F32)
        xhi = sb("xhi", [P, CHUNKS, CHUNK], F32R)
        xlo = sb("xlo", [P, CHUNKS, CHUNK], F32R)
        moe_hi = sb("moe_hi", [P, 2, EXPERTS * F], F32R)
        moe_lo = sb("moe_lo", [P, 2, EXPERTS * F], F32R)
        ffn_hi = sb("ffn_hi", [P, FFN_PIECES, F], F32R)
        ffn_lo = sb("ffn_lo", [P, FFN_PIECES, F], F32R)
        lang_hi = sb("lang_hi", [P, BATCHES, D], F32R)
        lang_lo = sb("lang_lo", [P, BATCHES, D], F32R)
        hid_hi = sb("hid_hi", [P, 3, FC, CHUNK], F32R)
        hid_lo = sb("hid_lo", [P, 3, FC, CHUNK], F32R)
        act_out = sb("act_out", [P, 2, 2, CHUNK], F32)
        cw_all = sb("cw_all", [P, 2, EXPERTS, CHUNK], F32)
        prod = sb("prod", [P, 2, CHUNK], F32)
        stage = sb("stage", [P, RING * F], F32)
        vec = sb("vec", [P, V_N], F32)
        emb = sb("emb", [P, BATCHES], F32)
        gbias = sb("gbias", [P, ROUNDS * EXPERTS], F32)
        ids = sb("ids", [1, 2 * BATCHES], I32)
        ident = sb("ident", [P, P], F32)
        upper = sb("upper", [P, EXPERTS, EXPERTS], F32)
        need = sb("need", [P, EXPERTS], F32)
        logit = sb("logit", [P, BLOCKS, EXPERTS], F32)
        beats = sb("beats", [P, BLOCKS, EXPERTS, EXPERTS], F32)
        beats_up = sb("beats_up", [P, BLOCKS, EXPERTS, EXPERTS], F32)
        net = sb("net", [P, BLOCKS, EXPERTS, EXPERTS], F32)
        wins = sb("wins", [P, BLOCKS, EXPERTS], F32)
        chosen = sb("chosen", [P, BLOCKS, EXPERTS], F32)
        top = sb("top", [P, BLOCKS], F32)
        below = sb("below", [P, BLOCKS, EXPERTS], F32)
        below_ch = sb("below_ch", [P, BLOCKS, EXPERTS], F32)
        second = sb("second", [P, BLOCKS], F32)
        half_gap = sb("half_gap", [P, BLOCKS, EXPERTS], F32)
        tanh_gap = sb("tanh_gap", [P, BLOCKS, EXPERTS], F32)
        cw_tok = sb("cw_tok", [P, EXPERTS, BLOCKS], F32)
        cw_row = sb("cw_row", [EXPERTS * BLOCKS, P], F32)
        cw_dram = nc.dram_tensor("cw_dram", [2, EXPERTS * CHUNK], F32).ap()

        base = cur[:, CHUNKS - 2:CHUNKS, :]
        lora = stage[:, 0:2 * LORA_W].rearrange("p (h n) -> p h n", h=2)
        lang_f = stage[:, 2 * LORA_W:].rearrange("p (h n) -> p h n", h=2)
        merged = act_out[:, 1, :, :]
        mer_hi = hid_hi[:, 2, :, :].rearrange("p (b m) f -> p b m f", b=2)
        mer_lo = hid_lo[:, 2, :, :].rearrange("p (b m) f -> p b m f", b=2)
        moe_raw = cw_all[:].rearrange("p s e t -> p s (e t)")
        ffn_raw = stage[:].rearrange("p (i f) -> p i f", f=F)

        bank = ctx.enter_context(nc.psum_tensor("bank", [P, 8, CHUNK], F32))
        MERGE, GATE = 6, 7

        x_in = [sem(f"x_in{c}") for c in range(CHUNKS)]
        ids_in, base_in, common_in, lang_in, small_in = (
            sem(n) for n in ("ids_in", "base_in", "common_in", "lang_in", "small_in"))
        lora_in = [sem(f"lora_in{b}") for b in range(BATCHES)]
        moe_in = [sem(f"moe_in{i}") for i in range(4)]
        ffn_in = [sem(f"ffn_in{i}") for i in range(2)]
        const_done = sem("const_done")
        x0_hi, x0_split = sem("x0_hi"), sem("x0_split")
        merge_done = sem("merge_done")
        lang_step = sem("lang_step")
        merge_free = sem("merge_free")
        mer_hi_done, mer_lo_done = sem("mer_hi_done"), sem("mer_lo_done")
        moe_hi_done, moe_lo_done = sem("moe_hi_done"), sem("moe_lo_done")
        cond_h_done = sem("cond_h_done")
        relu_hi, relu_lo = sem("relu_hi"), sem("relu_lo")
        cond_cur, cond_xhi = sem("cond_cur"), sem("cond_xhi")
        h_done = sem("h_done")
        g_done = sem("g_done")
        hi_done, lo_done = sem("hi_done"), sem("lo_done")
        y_done = sem("y_done")
        prod_done = sem("prod_done")
        add_done = sem("add_done")
        res_done = sem("res_done")
        xhi_done, xs_done = sem("xhi_done"), sem("xs_done")
        logit_done, gate_step, tanh_done = sem("logit_done"), sem("gate_step"), sem("tanh_done")
        cw_done, cw_turned, cw_copied, cw_stored = (
            sem(n) for n in ("cw_done", "cw_turned", "cw_copied", "cw_stored"))
        cw_ready = [sem(f"cw_ready{i}") for i in range(2)]
        ffn_hi_done, ffn_lo_done = sem("ffn_hi_done"), sem("ffn_lo_done")
        proj_done, z_hi = sem("proj_done"), sem("z_hi")
        evac_done = sem("evac_done")
        gated_done, silu_done = sem("gated_done"), sem("silu_done")
        o_done, gelu_done = sem("o_done"), sem("gelu_done")
        out_done = sem("out_done")

        block = ctx.enter_context(nc.Block())

        def lora_rows(b):
            return slice(32 * (b % 4), 32 * (b % 4) + 2 * RANK)

        def batch_cols(b):
            return slice(SEQ * (b % PER_CHUNK), SEQ * (b % PER_CHUNK) + SEQ)

        @block.sync
        def _(sp):
            sp.dma_start(ids[:, 0:BATCHES], ids0).then_inc(ids_in, 16)
            sp.dma_start(ids[:, BATCHES:], ids1).then_inc(ids_in, 16)
            for j in range(4):
                sp.dma_start(lora[32 * j:32 * j + RANK, :, :],
                             lora_common.unsqueeze(1).to_broadcast([RANK, 2, LORA_W])).then_inc(common_in, 16)
            sp.dma_start(base, cond_base).then_inc(base_in, 16)
            sp.wait_ge(ids_in, 32)
            for b in range(BATCHES):
                e = sp.value_load(ids[0:1, b:b + 1], min_val=0, max_val=LORA_EXPERTS - 1)
                sp.dma_start(lora[32 * (b % 4) + RANK:32 * (b % 4) + 2 * RANK, b // 4, :],
                             lora_expert[bass.ds(e, 1), :, :].rearrange("e r n -> (e r) n")).then_inc(lora_in[b], 16)
                if b < CHUNKS:
                    sp.dma_start(x0[:, b, :], x_t[:, b * CHUNK:(b + 1) * CHUNK]).then_inc(x_in[b], 16)
            sp.dma_start(vec[:], vecs).then_inc(small_in, 16)
            sp.dma_start(gbias[:], gate_bias.to_broadcast([P, ROUNDS * EXPERTS])).then_inc(small_in, 16)
            for i in range(4):
                half = slice((i % 2) * 2 * F, (i % 2 + 1) * 2 * F)
                sp.dma_start(moe_raw[:, i // 2, half], moe_w[:, i // 2, half]).then_inc(moe_in[i], 16)
            for b in range(BATCHES):
                e = sp.value_load(ids[0:1, BATCHES + b:BATCHES + b + 1], min_val=0, max_val=LANGS - 1)
                sp.dma_start(lang_f[32 * (b % 4):32 * (b % 4) + RANK, b // 4, :],
                             lang_lora[bass.ds(e, 1), :, :].rearrange("e r n -> (e r) n")).then_inc(lang_in, 16)
                sp.dma_start(emb[:, b:b + 1],
                             lang_embed[bass.ds(e, 1), :].rearrange("e d -> d e")).then_inc(lang_in, 16)

            def broadcast_gate(slot, copied, read, stored, gated):
                sp.wait_ge(cw_copied, copied)
                if read is not None:
                    sp.wait_ge(cw_ready[slot], read)
                sp.dma_start(cw_dram[slot:slot + 1, :].rearrange("s (r t) -> (s r) t", t=P), cw_row[:])\
                  .then_inc(cw_stored, 16)
                sp.wait_ge(cw_stored, stored)
                if gated is None:
                    sp.wait_ge(moe_lo_done, 4)
                else:
                    sp.wait_ge(add_done, gated)
                sp.dma_start(cw_all[:, slot, :, :].rearrange("p e t -> p (e t)"),
                             cw_dram[slot:slot + 1, :].to_broadcast([P, EXPERTS * CHUNK])).then_inc(cw_ready[slot], 16)

            for slot in range(2):
                broadcast_gate(slot, slot + 1, None, 16 * slot + 16, None)
            with sp.Fori(1, ROUNDS * CHUNKS // 2) as pair:
                read = sp.to_reg(16 * pair)
                counts = [(sp.to_reg(2 * pair + slot + 1), sp.to_reg(32 * pair + 16 * slot + 16),
                           sp.to_reg(2 * EXPERTS * pair + EXPERTS * (slot - 1) + ADD0)) for slot in range(2)]
                for slot, (copied, stored, gated) in enumerate(counts):
                    broadcast_gate(slot, copied, read, stored, gated)
            for c in range(CHUNKS):
                sp.wait_ge(evac_done, Z_ALL + c + 1)
                sp.dma_start(out_t[:, c * CHUNK:(c + 1) * CHUNK], x0[:, c, :]).then_inc(out_done, 16)
            sp.wait_ge(out_done, 16 * CHUNKS)

        @block.gpsimd
        def _(pool):
            pool.memset(ident[:], 0.0).then_inc(const_done, 1)
            pool.memset(upper[:], 1.0).then_inc(const_done, 1)
            for i in range(EXPERTS):
                pool.memset(need[:, i:i + 1], 2.0 - i).then_inc(const_done, 1)
            pool.wait_ge(const_done, 2 + EXPERTS)
            pool.affine_select(out=ident[:], in_=ident[:], compare_op=ALU.not_equal, fill=1.0, base=0,
                               pattern=[[-1, P]], channel_multiplier=1).then_inc(const_done, 1)
            pool.affine_select(out=upper[:], in_=upper[:], compare_op=ALU.is_gt, fill=0.0, base=0,
                               pattern=[[-1, EXPERTS], [1, EXPERTS]], channel_multiplier=0).then_inc(const_done, 1)
            pool.wait_ge(merge_done, MERGES)
            pool.dma_start(ffn_raw, ffn_w[:, 0:RING, :]).then_inc(ffn_in[0], 16)
            for i in range(FFN_PIECES):
                if i == FFN_PIECES - RING:
                    pool.wait_ge(ffn_lo_done, i)
                    pool.dma_start(ffn_raw[:, 0:i, :], ffn_w[:, RING:FFN_PIECES, :]).then_inc(ffn_in[1], 16)
                pool.wait_ge(ffn_hi_done, i + 1)
                pool.tensor_tensor(ffn_lo[:, i, :], ffn_raw[:, i % RING, :], ffn_hi[:, i, :].bitcast(F32),
                                   ALU.subtract).then_inc(ffn_lo_done, 1)

        @block.tensor
        def _(pe):
            def product(out, w_hi, w_lo, r_hi, r_lo, start, stop):
                pe.matmul(out, w_hi, r_hi, start=start, stop=False)
                pe.matmul(out, w_hi, r_lo, start=False, stop=False)
                return pe.matmul(out, w_lo, r_hi, start=False, stop=stop)

            def merge(m):
                if m >= 1:
                    pe.wait_ge(merge_free, m)
                if m >= 2 * BATCHES:
                    pe.wait_ge(lang_in, 32 * BATCHES)
                    half = m - 2 * BATCHES
                    for j in range(4):
                        rows = slice(32 * j, 32 * j + RANK)
                        if j:
                            pe.wait_ge(lang_step, 3 * half + j)
                        pe.matmul(bank[:, MERGE, j * D:(j + 1) * D], lang_f[rows, half, 0:D],
                                  lang_f[rows, half, D:2 * D], start=True, stop=True)\
                            .then_inc(lang_step if j < 3 else merge_done, 1)
                    return
                b, rows, half = m // 2, lora_rows(m // 2), m // 2 // 4
                pe.wait_ge(common_in, 64)
                pe.wait_ge(lora_in[b], 16)
                if m % 2 == 0:
                    pe.matmul(bank[:, MERGE, :], lora[rows, half, 0:D], lora[rows, half, D:D + F],
                              start=True, stop=True).then_inc(merge_done, 1)
                else:
                    for fc in range(FC):
                        a = D + F + fc * P
                        mm = pe.matmul(bank[:, MERGE, fc * D:(fc + 1) * D], lora[rows, half, a:a + P],
                                       lora[rows, half, D + 2 * F:LORA_W], start=True, stop=True)
                    mm.then_inc(merge_done, 1)

            def cond_hidden(b):
                pe.wait_ge(mer_lo_done, 2 * b + 1)
                pe.wait_ge(x0_split, b // PER_CHUNK + 1)
                if b >= 2:
                    pe.wait_ge(relu_lo, b - 1)
                cols = batch_cols(b)
                for f in range(FC):
                    w = slice(f * P, (f + 1) * P)
                    mm = product(bank[:, 2 * (b % 2) + f // 2, (f % 2) * SEQ:(f % 2 + 1) * SEQ],
                                 mer_hi[:, b % 2, 0, w], mer_lo[:, b % 2, 0, w],
                                 xhi[:, b // PER_CHUNK, cols], xlo[:, b // PER_CHUNK, cols], True, True)
                mm.then_inc(cond_h_done, 1)

            def cond_out(b):
                c = b // PER_CHUNK
                pe.wait_ge(mer_lo_done, 2 * b + 2)
                pe.wait_ge(relu_lo, b + 1)
                if c >= 2 and b % PER_CHUNK == 0:
                    pe.wait_ge(xs_done, c - 1)
                for fc in range(FC):
                    w = slice(fc * D, (fc + 1) * D)
                    r = slice((fc % 2) * SEQ, (fc % 2 + 1) * SEQ)
                    mm = product(bank[:, 4 + c % 2, batch_cols(b)], mer_hi[:, b % 2, 1, w], mer_lo[:, b % 2, 1, w],
                                 hid_hi[:, b % 2, fc // 2, r], hid_lo[:, b % 2, fc // 2, r], fc == 0, fc == FC - 1)
                mm.then_inc(y_done, 1)

            def logits(c, rnd):
                for t in range(BLOCKS):
                    mm = pe.matmul(bank[:, GATE, t * EXPERTS:(t + 1) * EXPERTS], cur[:, c, t * P:(t + 1) * P],
                                   vec[:, bass.ds(V_WG + EXPERTS * rnd, EXPERTS)], start=True, stop=True)
                mm.then_inc(logit_done, 1)

            def turn_gate(q):
                pe.wait_ge(cw_done, q + 1)
                pe.transpose(bank[0:EXPERTS * BLOCKS, GATE, P:2 * P], cw_tok[:].rearrange("p e t -> p (e t)"),
                             ident[:]).then_inc(cw_turned, 1)

            def expert_in(n, s, rnd):
                c, e = s // EXPERTS, s % EXPERTS
                if e == 0:
                    pe.wait_ge(xs_done, CHUNKS * rnd + c + 1)
                for f in range(FC):
                    if s != 0 or not isinstance(rnd, int) or rnd:
                        pe.wait_ge(g_done, FC * n + f - 3)
                    w = slice(e * F + f * P, e * F + (f + 1) * P)
                    product(bank[:, f, :], moe_hi[:, 0, w], moe_lo[:, 0, w], xhi[:, c, :], xlo[:, c, :],
                            True, True).then_inc(h_done, 1)

            def expert_out(n, s):
                e = s % EXPERTS
                pe.wait_ge(add_done, n + 1)
                for fc in range(FC):
                    if fc % 2 == 0:
                        pe.wait_ge(lo_done, 2 * n + fc // 2 + 1)
                    w = slice(e * F + fc * D, e * F + (fc + 1) * D)
                    mm = product(bank[:, 4 + s % 2, :], moe_hi[:, 1, w], moe_lo[:, 1, w],
                                 hid_hi[:, s % 2, fc, :], hid_lo[:, s % 2, fc, :], fc == 0, fc == FC - 1)
                mm.then_inc(y_done, 1)

            def project(c):
                pe.wait_ge(xs_done, CHUNKS * ROUNDS + c + 1)
                if c == 0:
                    pe.wait_ge(cw_copied, CHUNKS * ROUNDS)
                    pe.wait_ge(mer_lo_done, MERGES)
                else:
                    pe.wait_ge(evac_done, 2 * c)
                for j in range(PER_CHUNK):
                    b, t = PER_CHUNK * c + j, slice(j * SEQ, (j + 1) * SEQ)
                    mm = product(bank[:, GATE, t], lang_hi[:, b, :], lang_lo[:, b, :], xhi[:, c, t], xlo[:, c, t],
                                 True, True)
                mm.then_inc(proj_done, 1)

            def round_steps(rnd, last):
                for s in range(STEPS):
                    n = STEPS * rnd + s
                    if s < STEPS - 1:
                        expert_in(n + 1, s + 1, rnd)
                    elif not last:
                        expert_in(n + 1, 0, rnd + 1)
                    c = s // EXPERTS - 1
                    if s == 0:
                        pe.wait_ge(add_done, ADD0 + n)
                        pe.wait_ge(cw_copied, CHUNKS * rnd + CHUNKS - 1)
                        logits(CHUNKS - 1, rnd)
                    elif s == 1:
                        turn_gate(CHUNKS * rnd + CHUNKS - 1)
                    elif s % EXPERTS == 0 and not last:
                        pe.wait_ge(add_done, ADD0 + n)
                        pe.wait_ge(cw_copied, CHUNKS * (rnd + 1) + c)
                        logits(c, rnd + 1)
                    elif s % EXPERTS == 1:
                        if last:
                            project(c)
                        else:
                            turn_gate(CHUNKS * (rnd + 1) + c)
                    expert_out(n, s)

            pe.wait_ge(const_done, 4 + EXPERTS)
            pe.wait_ge(small_in, 32)
            merge(0)
            merge(1)
            cond_hidden(0)
            merge(2)
            merge(3)
            for b in range(BATCHES):
                if b + 1 < BATCHES:
                    cond_hidden(b + 1)
                if 2 * b + 4 < MERGES:
                    merge(2 * b + 4)
                if b % 2 == 0 and b >= 2:
                    c = b // 2 - 1
                    pe.wait_ge(xs_done, c + 1)
                    if c >= 1:
                        pe.wait_ge(cw_copied, c)
                    logits(c, 0)
                elif b % 2 == 1 and b >= 3:
                    turn_gate(b // 2 - 1)
                cond_out(b)
                if 2 * b + 5 < MERGES:
                    merge(2 * b + 5)

            pe.wait_ge(moe_lo_done, 4)
            pe.wait_ge(relu_lo, BATCHES)
            expert_in(0, 0, 0)
            with pe.Fori(0, ROUNDS - 1) as rnd:
                round_steps(rnd, False)
            round_steps(ROUNDS - 1, True)
            project(CHUNKS - 1)

            pe.wait_ge(ffn_lo_done, FFN_PIECES)
            with pe.Fori(0, PAIRS) as pair:
                for j in range(2):
                    if j == 0:
                        pe.wait_ge(evac_done, Z_ALL + 2 * pair)
                    for f in range(FC):
                        if j == 1:
                            pe.wait_ge(add_done, ADD_MOE + 8 * pair + f + 1)
                        w = slice(f * P, (f + 1) * P)
                        z = bass.ds(2 * pair + j, 1)
                        z_h = xhi[:, z, :].rearrange("p c t -> p (c t)")
                        z_l = xlo[:, z, :].rearrange("p c t -> p (c t)")
                        product(bank[:, 2 * f, :], ffn_hi[:, 0, w], ffn_lo[:, 0, w], z_h, z_l, True, True)
                        product(bank[:, 2 * f + 1, :], ffn_hi[:, 1, w], ffn_lo[:, 1, w], z_h, z_l, True, True)\
                            .then_inc(gated_done, 1)
                for k in range(2, 6):
                    src, piece = (k - 2) % 3, 2 if k < 4 else 2 + FC
                    for o in range(FC):
                        if k < 4:
                            pe.wait_ge(add_done, ADD_MOE + 8 * pair + 4 + 2 * (k - 2) + o // 2 + 1)
                        else:
                            pe.wait_ge(gelu_done, 16 * pair + FC * (k - 4) + o + 1)
                        for i in range(FC):
                            if o == 0 and i % 2 == 0:
                                pe.wait_ge(lo_done, LO_MOE + 12 * pair + 2 * (k - 2) + i // 2 + 1)
                            w = slice(o * P, (o + 1) * P)
                            mm = product(bank[:, o + 4 * (k % 2), :], ffn_hi[:, piece + i, w], ffn_lo[:, piece + i, w],
                                         hid_hi[:, src, i, :], hid_lo[:, src, i, :], i == 0, i == FC - 1)
                        mm.then_inc(o_done, 1)
                for j in range(2):
                    pe.wait_ge(gelu_done, 16 * pair + 8 + 4 * j + 1)
                    for i in range(FC):
                        if i % 2 == 0:
                            pe.wait_ge(lo_done, LO_MOE + 12 * pair + 2 * (4 + j) + i // 2 + 1)
                        w = slice(i * P, (i + 1) * P)
                        mm = product(bank[:, 4 * j, :], ffn_hi[:, FFN_PIECES - 1, w], ffn_lo[:, FFN_PIECES - 1, w],
                                     hid_hi[:, 1 + j, i, :], hid_lo[:, 1 + j, i, :], i == 0, i == FC - 1)
                    mm.then_inc(y_done, 1)

        @block.scalar
        def _(act):
            def merged_high(m):
                if m >= 2 * BATCHES:
                    act.wait_ge(merge_done, m + 1)
                    half = m - 2 * BATCHES
                    act.activation(lang_hi[:, 4 * half:4 * half + 4, :].rearrange("p b d -> p (b d)"),
                                   bank[:, MERGE, :], ACT.Copy).then_inc(mer_hi_done, 1)
                    return
                b = m // 2
                act.wait_ge(merge_free, m + 1)
                if b >= 2 and m % 2 == 0:
                    act.wait_ge(cond_h_done, b - 1)
                if b >= 2 and m % 2 == 1:
                    act.wait_ge(y_done, b - 1)
                act.activation(mer_hi[:, b % 2, m % 2, :], merged[:, m % 2, :], ACT.Copy).then_inc(mer_hi_done, 1)

            def tanh_gate(q):
                act.wait_ge(gate_step, GATE_OPS * q + GATE_OPS)
                act.activation(tanh_gap[:], half_gap[:], ACT.Tanh).then_inc(tanh_done, 1)

            def copy_gate(q, first):
                act.wait_ge(cw_turned, q + 1)
                if not first:
                    act.wait_ge(cw_stored, 16 * q)
                act.activation(cw_row[:], bank[0:EXPERTS * BLOCKS, GATE, P:2 * P], ACT.Copy, scale=0.5)\
                   .then_inc(cw_copied, 1)

            def hidden(n, s, first=False):
                e = s % EXPERTS
                for f in range(FC):
                    if f % 2 == 0 and not first:
                        act.wait_ge(lo_done, 2 * n + f // 2 - 1)
                    act.wait_ge(h_done, FC * n + f + 1)
                    act.activation(act_out[:, f // 2, f % 2, :], bank[:, f, :], ACT.Gelu_apprx_tanh,
                                   bias=vec[:, V_B1 + e * FC + f:V_B1 + e * FC + f + 1]).then_inc(g_done, 1)
                    if f % 2 == 1:
                        if f == 1:
                            act.wait_ge(y_done, Y_COND if first else n + Y_COND - 1)
                        act.wait_ge(g_done, FC * n + f + 1)
                        act.activation(hid_hi[:, s % 2, f - 1:f + 1, :], act_out[:, f // 2, :, :], ACT.Copy)\
                           .then_inc(hi_done, 1)

            def project_high(c):
                act.wait_ge(proj_done, c + 1)
                for j in range(PER_CHUNK):
                    b, t = PER_CHUNK * c + j, slice(j * SEQ, (j + 1) * SEQ)
                    act.activation(xhi[:, c, t], bank[:, GATE, t], ACT.Identity, bias=emb[:, b:b + 1])\
                       .then_inc(z_hi, 1)

            def round_steps(rnd, last):
                for s in range(STEPS):
                    n = STEPS * rnd + s
                    if s < STEPS - 1:
                        hidden(n + 1, s + 1)
                    elif not last:
                        hidden(n + 1, 0)
                    c = s // EXPERTS - 1
                    if s == 0:
                        tanh_gate(CHUNKS * rnd + CHUNKS - 1)
                    elif s == 1:
                        copy_gate(CHUNKS * rnd + CHUNKS - 1, False)
                    elif s % EXPERTS == 0 and not last:
                        tanh_gate(CHUNKS * (rnd + 1) + c)
                    elif s % EXPERTS == 1:
                        if last:
                            project_high(c)
                        else:
                            copy_gate(CHUNKS * (rnd + 1) + c, False)
                    if last and s < FFN_PIECES:
                        act.wait_ge(ffn_in[s // RING], 16)
                        act.activation(ffn_hi[:, s, :], ffn_raw[:, s % RING, :], ACT.Copy).then_inc(ffn_hi_done, 1)

            for m in range(4):
                merged_high(m)
            for b in range(BATCHES):
                act.wait_ge(cond_h_done, b + 1)
                if b >= 2:
                    act.wait_ge(y_done, b - 1)
                act.activation(hid_hi[:, b % 2, 0:2, :], bank[:, 2 * (b % 2):2 * (b % 2) + 2, :], ACT.Relu)\
                   .then_inc(relu_hi, 1)
                for m in range(2 * b + 4, min(2 * b + 6, MERGES)):
                    merged_high(m)
                if b % 2 == 1:
                    c = b // 2
                    act.wait_ge(y_done, b + 1)
                    if c >= CHUNKS - 2:
                        act.wait_ge(merge_free, 2 * BATCHES)
                    act.activation(cur[:, c, :], bank[:, 4 + c % 2, :], ACT.Copy).then_inc(cond_cur, 1)
                    act.activation(xhi[:, c, :], bank[:, 4 + c % 2, :], ACT.Copy).then_inc(cond_xhi, 1)
                if 2 <= b < 6:
                    i = b - 2
                    half = slice((i % 2) * 2 * F, (i % 2 + 1) * 2 * F)
                    act.wait_ge(moe_in[i], 16)
                    act.activation(moe_hi[:, i // 2, half], moe_raw[:, i // 2, half], ACT.Copy).then_inc(moe_hi_done, 1)
                if b % 2 == 0 and b >= 2:
                    tanh_gate(b // 2 - 1)
                elif b % 2 == 1 and b >= 3:
                    copy_gate(b // 2 - 1, b == 3)

            act.wait_ge(mer_lo_done, 2 * BATCHES)
            hidden(0, 0, True)
            with act.Fori(0, ROUNDS - 1) as rnd:
                round_steps(rnd, False)
            round_steps(ROUNDS - 1, True)
            project_high(CHUNKS - 1)

            with act.Fori(0, PAIRS) as pair:
                def high(k, pr):
                    if pr == 0:
                        if k < 3:
                            act.wait_ge(y_done, Y_MOE + 2 * pair - (k == 0))
                        else:
                            act.wait_ge(o_done, 16 * pair + FC * (k - 2))
                    if k < 2:
                        act.wait_ge(add_done, ADD_MOE + 8 * pair + FC * k + 2 * pr + 2)
                    else:
                        act.wait_ge(gelu_done, 16 * pair + FC * (k - 2) + 2 * pr + 2)
                    act.activation(hid_hi[:, k % 3, 2 * pr:2 * pr + 2, :], act_out[:, pr, :, :], ACT.Copy)\
                       .then_inc(hi_done, 1)

                for k in range(2):
                    for f in range(FC):
                        act.wait_ge(gated_done, 8 * pair + FC * k + f + 1)
                        act.wait_ge(add_done, ADD_MOE + 8 * pair + FC * k + f - 1)
                        act.activation(prod[:, f % 2, :], bank[:, 2 * f, :], ACT.Silu,
                                       scale=vec[:, V_S1 + f:V_S1 + f + 1]).then_inc(silu_done, 1)
                        if f >= 2:
                            high(k, f - 2)
                for k in range(2, 6):
                    v = V_H1 if k < 4 else V_H2
                    for o in range(FC):
                        act.wait_ge(o_done, 16 * pair + FC * (k - 2) + o + 1)
                        if o % 2 == 0:
                            act.wait_ge(lo_done, LO_MOE + 12 * pair + 2 * k + o // 2 - 1)
                        act.activation(act_out[:, o // 2, o % 2, :], bank[:, o + 4 * (k % 2), :], ACT.Gelu,
                                       scale=vec[:, v + o:v + o + 1]).then_inc(gelu_done, 1)
                        if o % 2 == 1:
                            high(k, o // 2)

        @block.vector
        def _(dve):
            def split_x0(c):
                dve.wait_ge(x_in[c], 16)
                dve.tensor_copy(xhi[:, c, :], x0[:, c, :]).then_inc(x0_hi, 1)
                dve.wait_ge(x0_hi, c + 1)
                dve.tensor_tensor(xlo[:, c, :], x0[:, c, :], xhi[:, c, :].bitcast(F32), ALU.subtract)\
                   .then_inc(x0_split, 1)

            def merged_low(m):
                if m >= 2 * BATCHES:
                    half = m - 2 * BATCHES
                    dve.wait_ge(mer_hi_done, m + 1)
                    dve.tensor_tensor(lang_lo[:, 4 * half:4 * half + 4, :].rearrange("p b d -> p (b d)"),
                                      bank[:, MERGE, :],
                                      lang_hi[:, 4 * half:4 * half + 4, :].rearrange("p b d -> p (b d)").bitcast(F32),
                                      ALU.subtract).then_inc(mer_lo_done, 1)
                    dve.wait_ge(mer_lo_done, m + 1)
                    dve.sem_inc(merge_free, 1)
                    return
                b = m // 2
                if m == 0:
                    dve.wait_ge(base_in, 16)
                dve.wait_ge(merge_done, m + 1)
                if m >= 2:
                    dve.wait_ge(mer_lo_done, m - 1)
                dve.scalar_tensor_tensor(merged[:, m % 2, :], bank[:, MERGE, :], COND_ALPHA, base[:, m % 2, :],
                                         ALU.mult, ALU.add).then_inc(merge_free, 1)
                dve.wait_ge(mer_hi_done, m + 1)
                dve.tensor_tensor(mer_lo[:, b % 2, m % 2, :], merged[:, m % 2, :],
                                  mer_hi[:, b % 2, m % 2, :].bitcast(F32), ALU.subtract).then_inc(mer_lo_done, 1)

            def gate_scores(c, rnd):
                q = CHUNKS * rnd + c
                at = GATE_OPS * q
                shape = [P, BLOCKS, EXPERTS, EXPERTS]
                dve.wait_ge(logit_done, q + 1)
                dve.tensor_tensor(logit[:], bank[:, GATE, 0:BLOCKS * EXPERTS].rearrange("p (t e) -> p t e", e=EXPERTS),
                                  gbias[:, bass.ds(EXPERTS * rnd, EXPERTS)].unsqueeze(1)
                                  .to_broadcast([P, BLOCKS, EXPERTS]), ALU.add).then_inc(gate_step, 1)
                dve.wait_ge(gate_step, at + 1)
                dve.tensor_tensor(beats[:], logit[:].unsqueeze(3).to_broadcast(shape),
                                  logit[:].unsqueeze(2).to_broadcast(shape), ALU.is_ge).then_inc(gate_step, 1)
                dve.tensor_reduce(top[:], logit[:], AX_X, ALU.max).then_inc(gate_step, 1)
                dve.wait_ge(gate_step, at + 2)
                dve.tensor_tensor(beats_up[:].rearrange("p t i j -> p t (i j)"),
                                  beats[:].rearrange("p t i j -> p t (i j)"),
                                  upper[:].rearrange("p i j -> p (i j)").unsqueeze(1)
                                  .to_broadcast([P, BLOCKS, EXPERTS * EXPERTS]), ALU.mult).then_inc(gate_step, 1)
                dve.wait_ge(gate_step, at + 3)
                dve.tensor_tensor(below[:], logit[:], top[:].unsqueeze(2).to_broadcast([P, BLOCKS, EXPERTS]),
                                  ALU.subtract).then_inc(gate_step, 1)
                dve.wait_ge(gate_step, at + 4)
                dve.tensor_tensor(net[:], beats_up[:], beats_up[:].rearrange("p t i j -> p t j i"),
                                  ALU.subtract).then_inc(gate_step, 1)
                dve.wait_ge(gate_step, at + 6)
                dve.tensor_reduce(wins[:], net[:], AX_X, ALU.add).then_inc(gate_step, 1)
                dve.wait_ge(gate_step, at + 7)
                dve.tensor_tensor(chosen[:], wins[:], need[:].unsqueeze(1).to_broadcast([P, BLOCKS, EXPERTS]),
                                  ALU.is_ge).then_inc(gate_step, 1)
                dve.wait_ge(gate_step, at + 8)
                dve.tensor_tensor(below_ch[:], below[:], chosen[:], ALU.mult).then_inc(gate_step, 1)
                dve.wait_ge(gate_step, at + 9)
                dve.tensor_reduce(second[:], below_ch[:], AX_X, ALU.add).then_inc(gate_step, 1)
                dve.wait_ge(gate_step, at + 10)
                dve.scalar_tensor_tensor(half_gap[:], second[:].unsqueeze(2).to_broadcast([P, BLOCKS, EXPERTS]),
                                         -0.5, below[:], ALU.mult, ALU.add).then_inc(gate_step, 1)

            def gate_weights(q):
                dve.wait_ge(tanh_done, q + 1)
                dve.scalar_tensor_tensor(cw_tok[:].rearrange("p e t -> p t e"), tanh_gap[:], 1.0, chosen[:],
                                         ALU.add, ALU.mult).then_inc(cw_done, 1)

            def hidden_low(n, s):
                for pr in range(2):
                    dve.wait_ge(hi_done, 2 * n + pr + 1)
                    dve.tensor_tensor(hid_lo[:, s % 2, 2 * pr:2 * pr + 2, :], act_out[:, pr, :, :],
                                      hid_hi[:, s % 2, 2 * pr:2 * pr + 2, :].bitcast(F32), ALU.subtract)\
                       .then_inc(lo_done, 1)

            def round_steps(rnd, last):
                for s in range(STEPS):
                    n, c, e = STEPS * rnd + s, s // EXPERTS, s % EXPERTS
                    if s == 1:
                        gate_weights(CHUNKS * rnd + CHUNKS - 1)
                    elif s % EXPERTS == 1 and not last:
                        gate_weights(CHUNKS * (rnd + 1) + c - 1)
                    if s == 0:
                        gate_scores(CHUNKS - 1, rnd)
                    elif s % EXPERTS == 0 and not last:
                        gate_scores(c - 1, rnd + 1)
                    if s < STEPS - 1:
                        hidden_low(n + 1, s + 1)
                    elif not last:
                        hidden_low(n + 1, 0)
                    if last and e == 1 and c >= 1:
                        project_low(c - 1)
                    if e == 0:
                        dve.wait_ge(cw_ready[c % 2], 16 * (2 * rnd + c // 2 + 1))
                    dve.wait_ge(y_done, Y_COND + n + 1)
                    dve.wait_ge(add_done, n + 1)
                    dve.scalar_tensor_tensor(prod[:, s % 2, :], bank[:, 4 + s % 2, :], vec[:, V_B2 + e:V_B2 + e + 1],
                                             cw_all[:, c % 2, e, :], ALU.add, ALU.mult).then_inc(prod_done, 1)
                    dve.wait_ge(prod_done, n + 1)
                    dve.wait_ge(add_done, ADD0 + n)
                    dve.tensor_tensor(cur[:, c, :], cur[:, c, :], prod[:, s % 2, :], ALU.add).then_inc(add_done, 1)
                    if e == EXPERTS - 1:
                        dve.wait_ge(add_done, ADD0 + n + 1)
                        if last:
                            dve.tensor_tensor(cur[:, c, :], cur[:, c, :], x0[:, c, :], ALU.add).then_inc(res_done, 1)
                            dve.wait_ge(res_done, c + 1)
                        dve.tensor_copy(xhi[:, c, :], cur[:, c, :]).then_inc(xhi_done, 1)
                        dve.wait_ge(xhi_done, CHUNKS * rnd + c + 1)
                        dve.tensor_tensor(xlo[:, c, :], cur[:, c, :], xhi[:, c, :].bitcast(F32), ALU.subtract)\
                           .then_inc(xs_done, 1)

            def project_low(c):
                dve.wait_ge(z_hi, PER_CHUNK * c + PER_CHUNK)
                for j in range(PER_CHUNK):
                    b, t = PER_CHUNK * c + j, slice(j * SEQ, (j + 1) * SEQ)
                    dve.scalar_tensor_tensor(xlo[:, c, t], bank[:, GATE, t], emb[:, b:b + 1],
                                             xhi[:, c, t].bitcast(F32), ALU.add, ALU.subtract).then_inc(evac_done, 1)

            split_x0(0)
            for m in range(4):
                merged_low(m)
            for b in range(BATCHES):
                if b % 2 == 0 and b // 2 + 1 < CHUNKS:
                    split_x0(b // 2 + 1)
                dve.wait_ge(relu_hi, b + 1)
                dve.scalar_tensor_tensor(hid_lo[:, b % 2, 0:2, :], bank[:, 2 * (b % 2):2 * (b % 2) + 2, :], 0.0,
                                         hid_hi[:, b % 2, 0:2, :].bitcast(F32), ALU.max, ALU.subtract)\
                   .then_inc(relu_lo, 1)
                if b % 2 == 1 and b >= 3:
                    gate_weights(b // 2 - 1)
                for m in range(2 * b + 4, min(2 * b + 6, MERGES)):
                    merged_low(m)
                    if m == 2 * b + 4 and b % 2 == 0 and b >= 2:
                        gate_scores(b // 2 - 1, 0)
                if b % 2 == 1:
                    c = b // 2
                    dve.wait_ge(cond_cur, c + 1)
                    dve.wait_ge(cond_xhi, c + 1)
                    dve.tensor_tensor(xlo[:, c, :], bank[:, 4 + c % 2, :], xhi[:, c, :].bitcast(F32), ALU.subtract)\
                       .then_inc(xs_done, 1)
                if 2 <= b < 6:
                    i = b - 2
                    half = slice((i % 2) * 2 * F, (i % 2 + 1) * 2 * F)
                    dve.wait_ge(moe_hi_done, i + 1)
                    dve.tensor_tensor(moe_lo[:, i // 2, half], moe_raw[:, i // 2, half],
                                      moe_hi[:, i // 2, half].bitcast(F32), ALU.subtract).then_inc(moe_lo_done, 1)
            dve.wait_ge(xs_done, CHUNKS)
            for i in range(2):
                dve.memset(prod[:, i, :], 0.0).then_inc(add_done, 1)

            hidden_low(0, 0)
            with dve.Fori(0, ROUNDS - 1) as rnd:
                round_steps(rnd, False)
            round_steps(ROUNDS - 1, True)
            project_low(CHUNKS - 1)

            with dve.Fori(0, PAIRS) as pair:
                def low(k, pr):
                    dve.wait_ge(hi_done, LO_MOE + 12 * pair + 2 * k + pr + 1)
                    dve.tensor_tensor(hid_lo[:, k % 3, 2 * pr:2 * pr + 2, :], act_out[:, pr, :, :],
                                      hid_hi[:, k % 3, 2 * pr:2 * pr + 2, :].bitcast(F32), ALU.subtract)\
                       .then_inc(lo_done, 1)

                for k in range(2):
                    for f in range(FC):
                        dve.wait_ge(silu_done, 8 * pair + FC * k + f + 1)
                        dve.wait_ge(lo_done, LO_MOE + 12 * pair + 2 * k + f // 2 - 1)
                        dve.scalar_tensor_tensor(act_out[:, f // 2, f % 2, :], bank[:, 2 * f + 1, :],
                                                 vec[:, V_S2 + f:V_S2 + f + 1], prod[:, f % 2, :],
                                                 ALU.mult, ALU.mult).then_inc(add_done, 1)
                        if f >= 2:
                            low(k, f - 2)
                for k in range(2, 6):
                    for pr in range(2):
                        low(k, pr)
                for j in range(2):
                    c = bass.ds(2 * pair + j, 1)
                    dve.wait_ge(y_done, Y_MOE + 2 * pair + j + 1)
                    dve.scalar_tensor_tensor(x0[:, c, :].rearrange("p c t -> p (c t)"), bank[:, 4 * j, :],
                                             vec[:, V_S3:V_S3 + 1], cur[:, c, :].rearrange("p c t -> p (c t)"),
                                             ALU.mult, ALU.add).then_inc(evac_done, 1)


def kernel(**inputs):
    import numpy as np
    import concourse.bacc as bacc
    from concourse.bass_utils import run_bass_kernel_spmd

    a = {k: np.asarray(v) for k, v in inputs.items()}

    def down(w):
        return w.T.reshape(-1, P, w.shape[0]).transpose(1, 0, 2)

    def cols(v):
        return v.reshape(-1, P).T

    def factors(ia, ib, oa, ob):
        return np.concatenate([ia, np.swapaxes(ib, -1, -2), oa, np.swapaxes(ob, -1, -2)], axis=-1)

    c, f, g = "L0_cond_", "L0_ffn_", "L1_ffn_"
    arrays = {
        "x_t": a["x"].reshape(TOKENS, D).T,
        "ids0": a["itok_B_0_7"].reshape(1, BATCHES),
        "ids1": a["itok_B_0_3"].reshape(1, BATCHES),
        "cond_base": np.stack([a[c + "wi"].T, down(a[c + "wo"]).reshape(P, F)], axis=1),
        "lora_common": factors(a[c + "common_wi_a"], a[c + "common_wi_b"], a[c + "common_wo_a"], a[c + "common_wo_b"]),
        "lora_expert": factors(a[c + "experts_wi_a"], a[c + "experts_wi_b"], a[c + "experts_wo_a"],
                               a[c + "experts_wo_b"]),
        "lang_lora": np.concatenate([a["L1_cond_lora_A"], np.swapaxes(a["L1_cond_lora_B"], 1, 2)], axis=2),
        "lang_embed": a["L1_cond_lang_embed"],
        "moe_w": np.stack([a[f + "W1"].transpose(1, 0, 2).reshape(P, EXPERTS * F),
                           a[f + "W2"].reshape(EXPERTS * FC, P, D).transpose(1, 0, 2).reshape(P, EXPERTS * F)], axis=1),
        "vecs": np.concatenate([cols(a[f + "b1"]), cols(a[f + "b2"]), cols(a[g + "w1_s"]), cols(a[g + "w2_s"]),
                                cols(a[g + "h1_s"]), cols(a[g + "h2_s"]), cols(a[g + "w3_s"]),
                                a[f + "Wg"].transpose(1, 0, 2).reshape(P, ROUNDS * EXPERTS)], axis=1),
        "gate_bias": a[f + "bg"].reshape(1, ROUNDS * EXPERTS),
        "ffn_w": np.concatenate([a[g + "w1_w"].T[:, None, :], a[g + "w2_w"].T[:, None, :], down(a[g + "h1_w"]),
                                 down(a[g + "h2_w"]), down(a[g + "w3_w"]).reshape(P, 1, F)], axis=1),
    }
    arrays = {k: np.ascontiguousarray(v) for k, v in arrays.items()}
    nc = bacc.Bacc("TRN2", target_bir_lowering=False, num_devices=1)
    args = [nc.dram_tensor(k, v.shape, mybir.dt.from_np(v.dtype), kind="ExternalInput").ap()
            for k, v in arrays.items()]
    out = nc.dram_tensor("out_t", (P, TOKENS), F32, kind="ExternalOutput").ap()
    adaln_ffn(nc, *args, out)
    r = run_bass_kernel_spmd(nc, [arrays], core_ids=[0])
    return np.ascontiguousarray(r.results[0]["out_t"].T).reshape(BATCHES, SEQ, D)
```

```python
from contextlib import ExitStack

import concourse.bass as bass
from concourse import mybir

ACT = mybir.ActivationFunctionType
ALU = mybir.AluOpType
AX_X = mybir.AxisListType.X
F32 = mybir.dt.float32
F32R = mybir.dt.float32r
I32 = mybir.dt.int32

P = 128
BATCHES, SEQ, D = 8, 256, 128
TOKENS = BATCHES * SEQ
CHUNK = 512
CHUNKS = TOKENS // CHUNK
PER_CHUNK = CHUNK // SEQ
F = 512
FC = F // P
RANK = 16
LORA_EXPERTS, LANGS = 8, 4
COND_ALPHA = 2.0
EXPERTS, ROUNDS = 4, 4
STEPS = CHUNKS * EXPERTS
BLOCKS = CHUNK // P
EARLY = 6
AHEAD = 4
LORA_W = D + F + F + D
MOE_AT = {0: [0], 1: [1], 2: [2], 3: [3], 4: [4], 5: [5], 6: [6, 7]}
FFN_PIECES = 3 + 2 * FC
WARM = 11
RING = 6
MOE_PIECES = 2 * EXPERTS * F // F

V_B1, V_B2, V_S1, V_S2, V_H1, V_H2, V_S3, V_WG = 0, 16, 20, 24, 28, 32, 36, 37
V_N = V_WG + ROUNDS * EXPERTS

MERGES = 2 * BATCHES + 2
Y_COND = BATCHES
Y_MOE = Y_COND + ROUNDS * STEPS
ADD0 = 2
ADD_MOE = ADD0 + ROUNDS * STEPS
LO_MOE = 2 * ROUNDS * STEPS
Z_ALL = 2 * CHUNKS
GATE_OPS = 11


FFN_ORDER = [(1, 0), (1, 1), (0, 3), (2, 0), (2, 1), (3, 0), (3, 1), (1, 2), (4, 0), (1, 3), (4, 1),
             (2, 2), (2, 3), (3, 2), (3, 3), (4, 2), (4, 3)]


def split_at(stage, c):
    return [x for x in FFN_ORDER if 1 <= x[0] <= 3].index((stage, c))


def wide_at(stage, c):
    return [x for x in FFN_ORDER if 2 <= x[0] <= 3].index((stage, c))


def adaln_ffn(nc, x_t, batch_ids, cond_base, lora_all, lang_lora, lang_embed,
              moe_w, vecs, gate_bias, ffn_w, out_t):
    ctx = ExitStack()
    with ctx:
        def sb(name, shape, dt):
            return ctx.enter_context(nc.sbuf_tensor(name, shape, dt))

        def sem(name):
            return ctx.enter_context(nc.semaphore(name))

        x0 = sb("x0", [P, CHUNKS, CHUNK], F32)
        cur = sb("cur", [P, CHUNKS, CHUNK], F32)
        xhi = sb("xhi", [P, CHUNKS, CHUNK], F32R)
        xlo = sb("xlo", [P, CHUNKS, CHUNK], F32R)
        moe_hi = sb("moe_hi", [P, 2, EXPERTS * F], F32R)
        moe_lo = sb("moe_lo", [P, 2, EXPERTS * F], F32R)
        ffn_hi = sb("ffn_hi", [P, FFN_PIECES, F], F32R)
        ffn_lo = sb("ffn_lo", [P, FFN_PIECES, F], F32R)
        lang_hi = sb("lang_hi", [P, BATCHES, D], F32R)
        lang_lo = sb("lang_lo", [P, BATCHES, D], F32R)
        hid_hi = sb("hid_hi", [P, 3, FC, CHUNK], F32R)
        hid_lo = sb("hid_lo", [P, 3, FC, CHUNK], F32R)
        act_out = sb("act_out", [P, 2, 2, CHUNK], F32)
        cw_all = sb("cw_all", [P, 2, EXPERTS, CHUNK], F32)
        prod = sb("prod", [P, 2, CHUNK], F32)
        stage = sb("stage", [P, RING * F], F32)
        vec = sb("vec", [P, V_N], F32)
        low_max = sb("low_max", [P, FFN_PIECES], F32)
        low_row = sb("low_row", [P, 1], F32)
        low_any = sb("low_any", [P, 1], F32)
        emb = sb("emb", [P, BATCHES], F32)
        gbias = sb("gbias", [P, ROUNDS * EXPERTS], F32)
        ids = sb("ids", [1, 2 * BATCHES], I32)
        ident = sb("ident", [P, P], F32)
        upper = sb("upper", [P, EXPERTS, EXPERTS], F32)
        need = sb("need", [P, EXPERTS], F32)
        logit = sb("logit", [P, BLOCKS, EXPERTS], F32)
        beats = sb("beats", [P, BLOCKS, EXPERTS, EXPERTS], F32)
        beats_up = sb("beats_up", [P, BLOCKS, EXPERTS, EXPERTS], F32)
        net = sb("net", [P, BLOCKS, EXPERTS, EXPERTS], F32)
        wins = sb("wins", [P, BLOCKS, EXPERTS], F32)
        chosen = sb("chosen", [P, BLOCKS, EXPERTS], F32)
        top = sb("top", [P, BLOCKS], F32)
        below = sb("below", [P, BLOCKS, EXPERTS], F32)
        below_ch = sb("below_ch", [P, BLOCKS, EXPERTS], F32)
        second = sb("second", [P, BLOCKS], F32)
        half_gap = sb("half_gap", [P, BLOCKS, EXPERTS], F32)
        tanh_gap = sb("tanh_gap", [P, BLOCKS, EXPERTS], F32)
        cw_tok = sb("cw_tok", [P, EXPERTS, BLOCKS], F32)
        cw_row = sb("cw_row", [EXPERTS * BLOCKS, P], F32)
        cw_dram = nc.dram_tensor("cw_dram", [2, EXPERTS * CHUNK], F32).ap()

        base = cur[:, CHUNKS - 2:CHUNKS, :]
        lora = stage[:, 0:2 * LORA_W].rearrange("p (h n) -> p h n", h=2)
        lang_f = [at.rearrange("p h (b n) -> p (h b) n", n=2 * D) for at in (act_out[:, 0, :, :], prod[:])]
        merged = act_out[:, 1, :, :]
        mer_hi = ffn_hi[:, 0:2 * AHEAD, :].rearrange("p (b m) f -> p b m f", m=2)
        mer_lo = ffn_lo[:, 0:2 * AHEAD, :].rearrange("p (b m) f -> p b m f", m=2)
        moe_raw = cw_all[:].rearrange("p s e t -> p s (e t)")
        ffn_raw = stage[:].rearrange("p (i f) -> p i f", f=F)

        bank = ctx.enter_context(nc.psum_tensor("bank", [P, 8, CHUNK], F32))
        MERGE, GATE, LAST, OUT = 6, 7, 3, 2

        x_in = [sem(f"x_in{c}") for c in range(CHUNKS)]
        ids_in, base_in, lang_in, small_in = (sem(n) for n in ("ids_in", "base_in", "lang_in", "small_in"))
        lora_in = [sem(f"lora_in{b}") for b in range(BATCHES)]
        moe_in = [sem(f"moe_in{i}") for i in range(4)]
        ffn_in = [sem(f"ffn_in{i}") for i in range(2)]
        const_done = sem("const_done")
        x0_hi, x0_split = sem("x0_hi"), sem("x0_split")
        merge_done = sem("merge_done")
        merge_free = sem("merge_free")
        mer_hi_done, mer_lo_done = sem("mer_hi_done"), sem("mer_lo_done")
        moe_hi_done, moe_lo_done = sem("moe_hi_done"), sem("moe_lo_done")
        cond_h_done = sem("cond_h_done")
        relu_hi, relu_lo = sem("relu_hi"), sem("relu_lo")
        cond_cur, cond_xhi = sem("cond_cur"), sem("cond_xhi")
        h_done = sem("h_done")
        g_done = sem("g_done")
        hi_done, lo_done = sem("hi_done"), sem("lo_done")
        y_done = sem("y_done")
        prod_done = sem("prod_done")
        add_done = sem("add_done")
        res_done = sem("res_done")
        xhi_done, xs_done = sem("xhi_done"), sem("xs_done")
        logit_done, gate_step, tanh_done = sem("logit_done"), sem("gate_step"), sem("tanh_done")
        cw_done, cw_turned, cw_copied, cw_stored = (
            sem(n) for n in ("cw_done", "cw_turned", "cw_copied", "cw_stored"))
        cw_ready = [sem(f"cw_ready{i}") for i in range(2)]
        ffn_hi_done, ffn_lo_done = sem("ffn_hi_done"), sem("ffn_lo_done")
        low_max_done, low_any_done = sem("low_max_done"), sem("low_any_done")
        proj_done, z_hi = sem("proj_done"), sem("z_hi")
        evac_done = sem("evac_done")
        gated_done, silu_done = sem("gated_done"), sem("silu_done")
        o_done, gelu_done = sem("o_done"), sem("gelu_done")
        out_done = sem("out_done")

        block = ctx.enter_context(nc.Block())

        def lora_rows(b):
            return slice(32 * (b % 4), 32 * (b % 4) + 2 * RANK)

        def merge_bank(m):
            return GATE if m < EARLY and m % 2 == 1 else MERGE

        def project_bank(c):
            return LAST if c == CHUNKS - 1 else GATE

        def out_bank(c):
            return OUT + 4 * (c == CHUNKS - 1)

        def batch_cols(b):
            return slice(SEQ * (b % PER_CHUNK), SEQ * (b % PER_CHUNK) + SEQ)

        @block.sync
        def _(sp):
            sp.dma_start(ids[:], batch_ids).then_inc(ids_in, 16)
            sp.dma_start(x0[:, 0, :], x_t[:, 0:CHUNK]).then_inc(x_in[0], 16)
            sp.dma_start(base, cond_base).then_inc(base_in, 16)
            sp.wait_ge(ids_in, 16)
            for b in range(BATCHES):
                e = sp.value_load(ids[0:1, b:b + 1], min_val=0, max_val=LORA_EXPERTS - 1)
                sp.dma_start(lora[lora_rows(b), b // 4, :],
                             lora_all[bass.ds(e, 1), :, :].rearrange("e r n -> (e r) n")).then_inc(lora_in[b], 16)
                if b % 2 == 1 and b // 2 + 1 < CHUNKS:
                    c = b // 2 + 1
                    sp.dma_start(x0[:, c, :], x_t[:, c * CHUNK:(c + 1) * CHUNK]).then_inc(x_in[c], 16)
            sp.dma_start(vec[:], vecs).then_inc(small_in, 16)
            sp.dma_start(gbias[:], gate_bias.to_broadcast([P, ROUNDS * EXPERTS])).then_inc(small_in, 16)
            for b in range(BATCHES):
                e = sp.value_load(ids[0:1, BATCHES + b:BATCHES + b + 1], min_val=0, max_val=LANGS - 1)
                sp.dma_start(lang_f[b // 4][0:RANK, b % 4, :],
                             lang_lora[bass.ds(e, 1), :, :].rearrange("e r n -> (e r) n")).then_inc(lang_in, 16)
                sp.dma_start(emb[:, b:b + 1],
                             lang_embed[bass.ds(e, 1), :].rearrange("e d -> d e")).then_inc(lang_in, 16)

            def store_gate(slot, copied, read, stored):
                sp.wait_ge(cw_copied, copied)
                if read is not None:
                    sp.wait_ge(cw_ready[slot], read)
                sp.dma_start(cw_dram[slot:slot + 1, :].rearrange("s (r t) -> (s r) t", t=P), cw_row[:])\
                  .then_inc(cw_stored, 16)
                sp.wait_ge(cw_stored, stored)

            def broadcast_gate(slot):
                sp.dma_start(cw_all[:, slot, :, :].rearrange("p e t -> p (e t)"),
                             cw_dram[slot:slot + 1, :].to_broadcast([P, EXPERTS * CHUNK])).then_inc(cw_ready[slot], 16)

            for slot in range(2):
                store_gate(slot, slot + 1, None, 16 * slot + 16)
            sp.wait_ge(moe_lo_done, MOE_PIECES)
            for slot in range(2):
                broadcast_gate(slot)
            with sp.Fori(1, ROUNDS * CHUNKS // 2) as pair:
                read = sp.to_reg(16 * pair)
                counts = [(sp.to_reg(2 * pair + slot + 1), sp.to_reg(32 * pair + 16 * slot + 16),
                           sp.to_reg(2 * EXPERTS * pair + EXPERTS * (slot - 1) + ADD0)) for slot in range(2)]
                for slot, (copied, stored, gated) in enumerate(counts):
                    store_gate(slot, copied, read, stored)
                    sp.wait_ge(add_done, gated)
                    broadcast_gate(slot)
            for c in range(CHUNKS):
                sp.wait_ge(evac_done, Z_ALL + c + 1)
                sp.dma_start(out_t[:, c * CHUNK:(c + 1) * CHUNK], x0[:, c, :]).then_inc(out_done, 16)
            sp.wait_ge(out_done, 16 * CHUNKS)

        @block.gpsimd
        def _(pool):
            pool.memset(ident[:], 0.0).then_inc(const_done, 1)
            pool.memset(upper[:], 1.0).then_inc(const_done, 1)
            for i in range(EXPERTS):
                pool.memset(need[:, i:i + 1], 2.0 - i).then_inc(const_done, 1)
            pool.wait_ge(const_done, 2 + EXPERTS)
            pool.affine_select(out=ident[:], in_=ident[:], compare_op=ALU.not_equal, fill=1.0, base=0,
                               pattern=[[-1, P]], channel_multiplier=1).then_inc(const_done, 1)
            pool.affine_select(out=upper[:], in_=upper[:], compare_op=ALU.is_gt, fill=0.0, base=0,
                               pattern=[[-1, EXPERTS], [1, EXPERTS]], channel_multiplier=0).then_inc(const_done, 1)
            for b in range(-1, BATCHES):
                for m in range(2 * b + 5 if b >= 0 else 0, min(2 * b + 7, 2 * BATCHES)):
                    pool.wait_ge(mer_hi_done, m + 1)
                    pool.tensor_tensor(mer_lo[:, m // 2 % AHEAD, m % 2, :], merged[:, m % 2, :],
                                       mer_hi[:, m // 2 % AHEAD, m % 2, :].bitcast(F32), ALU.subtract)\
                        .then_inc(mer_lo_done, 1)
                for i in MOE_AT.get(b, ()):
                    piece = slice((i % EXPERTS) * F, (i % EXPERTS + 1) * F)
                    pool.wait_ge(moe_hi_done, i + 1)
                    pool.tensor_tensor(moe_lo[:, i // EXPERTS, piece], moe_raw[:, i // EXPERTS, piece],
                                       moe_hi[:, i // EXPERTS, piece].bitcast(F32), ALU.subtract)\
                        .then_inc(moe_lo_done, 1)
            pool.wait_ge(merge_done, MERGES)
            pool.dma_start(ffn_raw, ffn_w[:, 0:RING, :]).then_inc(ffn_in[0], 16)
            for i in range(FFN_PIECES):
                if i == FFN_PIECES - RING:
                    pool.wait_ge(ffn_lo_done, i)
                    pool.dma_start(ffn_raw[:, 0:i, :], ffn_w[:, RING:FFN_PIECES, :]).then_inc(ffn_in[1], 16)
                pool.wait_ge(ffn_hi_done, i + 1)
                pool.tensor_tensor(ffn_lo[:, i, :], ffn_raw[:, i % RING, :], ffn_hi[:, i, :].bitcast(F32),
                                   ALU.subtract).then_inc(ffn_lo_done, 1)
            pool.wait_ge(low_max_done, FFN_PIECES + 1)
            pool.partition_all_reduce(low_any[:], low_row[:], P, bass.bass_isa.ReduceOp.max).then_inc(low_any_done, 1)

        @block.tensor
        def _(pe):
            def product(out, w_hi, w_lo, r_hi, r_lo, start, stop):
                pe.matmul(out, w_hi, r_hi, start=start, stop=False)
                mm = pe.matmul(out, w_hi, r_lo, start=False, stop=stop and w_lo is None)
                if w_lo is None:
                    return mm
                return pe.matmul(out, w_lo, r_hi, start=False, stop=stop)

            def merge(m):
                if m >= EARLY:
                    pe.wait_ge(merge_free, m)
                elif m >= 2:
                    pe.wait_ge(merge_free, m - 1)
                if m >= 2 * BATCHES:
                    pe.wait_ge(lang_in, 32 * BATCHES)
                    for j in range(4):
                        factors = lang_f[m - 2 * BATCHES][0:RANK, j, :]
                        mm = pe.matmul(bank[:, MERGE, j * D:(j + 1) * D], factors[:, 0:D], factors[:, D:2 * D],
                                       start=True, stop=True)
                    mm.then_inc(merge_done, 1)
                    return
                b, rows, half = m // 2, lora_rows(m // 2), m // 2 // 4
                pe.wait_ge(lora_in[b], 16)
                if m % 2 == 0:
                    pe.matmul(bank[:, merge_bank(m), :], lora[rows, half, 0:D], lora[rows, half, D:D + F],
                              start=True, stop=True).then_inc(merge_done, 1)
                else:
                    for fc in range(FC):
                        a = D + F + fc * P
                        mm = pe.matmul(bank[:, merge_bank(m), fc * D:(fc + 1) * D], lora[rows, half, a:a + P],
                                       lora[rows, half, D + 2 * F:LORA_W], start=True, stop=True)
                    mm.then_inc(merge_done, 1)

            def cond_hidden(b):
                pe.wait_ge(mer_lo_done, 2 * b + 1)
                pe.wait_ge(x0_split, b // PER_CHUNK + 1)
                if b >= 2:
                    pe.wait_ge(relu_lo, b - 1)
                cols = batch_cols(b)
                for f in range(FC):
                    w = slice(f * P, (f + 1) * P)
                    mm = product(bank[:, 2 * (b % 2) + f // 2, (f % 2) * SEQ:(f % 2 + 1) * SEQ],
                                 mer_hi[:, b % AHEAD, 0, w], mer_lo[:, b % AHEAD, 0, w],
                                 xhi[:, b // PER_CHUNK, cols], xlo[:, b // PER_CHUNK, cols], True, True)
                mm.then_inc(cond_h_done, 1)

            def cond_out(b):
                c = b // PER_CHUNK
                pe.wait_ge(mer_lo_done, 2 * b + 2)
                pe.wait_ge(relu_lo, b + 1)
                if c >= 2 and b % PER_CHUNK == 0:
                    pe.wait_ge(xs_done, c - 1)
                for fc in range(FC):
                    w = slice(fc * D, (fc + 1) * D)
                    r = slice((fc % 2) * SEQ, (fc % 2 + 1) * SEQ)
                    mm = product(bank[:, 4 + c % 2, batch_cols(b)], mer_hi[:, b % AHEAD, 1, w], mer_lo[:, b % AHEAD, 1, w],
                                 hid_hi[:, b % 2, fc // 2, r], hid_lo[:, b % 2, fc // 2, r], fc == 0, fc == FC - 1)
                mm.then_inc(y_done, 1)

            def logits(c, rnd):
                for t in range(BLOCKS):
                    mm = pe.matmul(bank[:, GATE, t * EXPERTS:(t + 1) * EXPERTS], cur[:, c, t * P:(t + 1) * P],
                                   vec[:, bass.ds(V_WG + EXPERTS * rnd, EXPERTS)], start=True, stop=True)
                mm.then_inc(logit_done, 1)

            def turn_gate(q):
                pe.wait_ge(cw_done, q + 1)
                pe.transpose(bank[0:EXPERTS * BLOCKS, GATE, P:2 * P], cw_tok[:].rearrange("p e t -> p (e t)"),
                             ident[:]).then_inc(cw_turned, 1)

            def expert_in(n, s, rnd):
                c, e = s // EXPERTS, s % EXPERTS
                if e == 0:
                    pe.wait_ge(xs_done, CHUNKS * rnd + c + 1)
                for f in range(FC):
                    if s != 0 or not isinstance(rnd, int) or rnd:
                        pe.wait_ge(g_done, FC * n + f - 3)
                    w = slice(e * F + f * P, e * F + (f + 1) * P)
                    product(bank[:, f, :], moe_hi[:, 0, w], moe_lo[:, 0, w], xhi[:, c, :], xlo[:, c, :],
                            True, True).then_inc(h_done, 1)

            def expert_out(n, s):
                e = s % EXPERTS
                pe.wait_ge(add_done, n + 1)
                for fc in range(FC):
                    if fc % 2 == 0:
                        pe.wait_ge(lo_done, 2 * n + fc // 2 + 1)
                    w = slice(e * F + fc * D, e * F + (fc + 1) * D)
                    mm = product(bank[:, 4 + s % 2, :], moe_hi[:, 1, w], moe_lo[:, 1, w],
                                 hid_hi[:, s % 2, fc, :], hid_lo[:, s % 2, fc, :], fc == 0, fc == FC - 1)
                mm.then_inc(y_done, 1)

            def project(c):
                pe.wait_ge(xs_done, CHUNKS * ROUNDS + c + 1)
                if c == 0:
                    pe.wait_ge(cw_copied, CHUNKS * ROUNDS)
                    pe.wait_ge(merge_free, MERGES)
                elif c < CHUNKS - 1:
                    pe.wait_ge(evac_done, 2 * c)
                else:
                    pe.wait_ge(add_done, ADD_MOE + FC + LAST // 2 + 1)
                for j in range(PER_CHUNK):
                    b, t = PER_CHUNK * c + j, slice(j * SEQ, (j + 1) * SEQ)
                    mm = product(bank[:, project_bank(c), t], lang_hi[:, b, :], lang_lo[:, b, :], xhi[:, c, t], xlo[:, c, t],
                                 True, True)
                mm.then_inc(proj_done, 1)

            def round_steps(rnd, last):
                for s in range(STEPS):
                    n = STEPS * rnd + s
                    if s < STEPS - 1:
                        expert_in(n + 1, s + 1, rnd)
                    elif not last:
                        expert_in(n + 1, 0, rnd + 1)
                    c = s // EXPERTS - 1
                    if s == 1:
                        pe.wait_ge(add_done, ADD0 + STEPS * rnd)
                        pe.wait_ge(cw_copied, CHUNKS * rnd + CHUNKS - 1)
                        logits(CHUNKS - 1, rnd)
                    elif s % EXPERTS == 1:
                        if last:
                            project(c)
                        else:
                            pe.wait_ge(add_done, ADD0 + n - 1)
                            pe.wait_ge(cw_copied, CHUNKS * (rnd + 1) + c)
                            logits(c, rnd + 1)
                    expert_out(n, s)
                    if s == 3:
                        turn_gate(CHUNKS * rnd + CHUNKS - 1)
                    elif s % EXPERTS == 3 and not last:
                        turn_gate(CHUNKS * (rnd + 1) + c)

            pe.wait_ge(const_done, 4 + EXPERTS)
            for i in range(WARM):
                pe.matmul(bank[:, GATE, 0:P], ident[:], ident[:], start=True, stop=True)
            for m in range(EARLY - 1):
                merge(m)
            cond_hidden(0)
            merge(EARLY - 1)
            for b in range(BATCHES):
                c = b // 2 - 1
                if b + 1 < BATCHES:
                    cond_hidden(b + 1)
                if b % 2 == 0 and c >= 1:
                    turn_gate(c - 1)
                if 2 * b + 6 < MERGES:
                    merge(2 * b + 6)
                cond_out(b)
                if b % 2 == 0 and c >= 0:
                    if c == 0:
                        pe.wait_ge(small_in, 32)
                    else:
                        pe.wait_ge(cw_copied, c)
                    pe.wait_ge(cond_cur, c + 1)
                    logits(c, 0)
                if 2 * b + 7 < MERGES:
                    merge(2 * b + 7)

            pe.wait_ge(moe_lo_done, MOE_PIECES)
            pe.wait_ge(relu_lo, BATCHES)
            expert_in(0, 0, 0)
            turn_gate(CHUNKS - 2)
            with pe.Fori(0, ROUNDS - 1) as rnd:
                round_steps(rnd, False)
            round_steps(ROUNDS - 1, True)

            def gated(c, w_lo):
                for f in range(FC):
                    if c == 0:
                        if f == 0:
                            pe.wait_ge(evac_done, Z_ALL - 2)
                        elif f == 2:
                            pe.wait_ge(add_done, ADD_MOE)
                    elif c == 2:
                        pe.wait_ge(gelu_done, FC * wide_at(3, f // 2) + 2 * (f % 2) + 2)
                        if f == 0:
                            pe.wait_ge(evac_done, Z_ALL)
                    else:
                        pe.wait_ge(add_done, ADD_MOE + FC * (c - 1) + f + 1)
                        if c == 3 and f == OUT // 2:
                            pe.wait_ge(evac_done, Z_ALL + 1)
                    w = slice(f * P, (f + 1) * P)
                    product(bank[:, 2 * f, :], ffn_hi[:, 0, w], w_lo and ffn_lo[:, 0, w], xhi[:, c, :], xlo[:, c, :],
                            True, True)
                    product(bank[:, 2 * f + 1, :], ffn_hi[:, 1, w], w_lo and ffn_lo[:, 1, w], xhi[:, c, :],
                            xlo[:, c, :], True, True).then_inc(gated_done, 1)

            def contract(out, piece, w, t, w_lo):
                for i in range(FC):
                    if i % 2 == 0:
                        pe.wait_ge(lo_done, LO_MOE + 2 * t + i // 2 + 1)
                    at, cols = piece(i, w)
                    mm = product(out, ffn_hi[:, at, cols], w_lo and ffn_lo[:, at, cols],
                                 hid_hi[:, t % 3, i, :], hid_lo[:, t % 3, i, :], i == 0, i == FC - 1)
                return mm

            def wide(stage, c, w_lo):
                for o in range(FC):
                    if stage == 2:
                        pe.wait_ge(add_done, ADD_MOE + FC * (c | 1) + 2 * (c % 2) + o // 2 + 1)
                        if c == 0 and o == LAST:
                            pe.wait_ge(evac_done, Z_ALL)
                        if c == 2 and o == OUT:
                            pe.wait_ge(evac_done, Z_ALL + 2)
                    else:
                        pe.wait_ge(gelu_done, FC * wide_at(2, c) + o + 1)
                    first = 2 + FC * (stage - 2)
                    contract(bank[:, o + 4 * (c % 2), :], lambda i, w: (first + i, w), slice(o * P, (o + 1) * P),
                             split_at(stage - 1, c), w_lo).then_inc(o_done, 1)

            def narrow(c, w_lo):
                if c < 2:
                    pe.wait_ge(add_done, ADD_MOE + FC * (c + 2) + OUT // 2 + 1)
                else:
                    pe.wait_ge(gelu_done, FC * wide_at(3, c) + OUT + 1)
                contract(bank[:, out_bank(c), :], lambda i, w: (FFN_PIECES - 1, slice(i * P, (i + 1) * P)), None,
                         split_at(3, c), w_lo).then_inc(y_done, 1)

            def ffn(w_lo):
                for stage, c in FFN_ORDER:
                    if stage == 0:
                        project(c)
                    elif stage == 1:
                        gated(c, w_lo)
                    elif stage < 4:
                        wide(stage, c, w_lo)
                    else:
                        narrow(c, w_lo)

            pe.wait_ge(low_any_done, 1)
            inexact = pe.alloc_register("inexact")
            pe.reg_load(inexact, low_any[0:1, 0:1].bitcast(I32))
            with pe.If_eq(inexact, 0):
                ffn(None)
            with pe.Else():
                ffn(True)

        @block.scalar
        def _(act):
            def merged_high(m):
                if m >= 2 * BATCHES:
                    act.wait_ge(merge_done, m + 1)
                    half = m - 2 * BATCHES
                    act.activation(lang_hi[:, 4 * half:4 * half + 4, :].rearrange("p b d -> p (b d)"),
                                   bank[:, MERGE, :], ACT.Copy).then_inc(mer_hi_done, 1)
                    return
                b = m // 2
                act.wait_ge(merge_free, m + 1)
                if b >= AHEAD:
                    act.wait_ge(cond_h_done if m % 2 == 0 else y_done, b - AHEAD + 1)
                act.activation(mer_hi[:, b % AHEAD, m % 2, :], merged[:, m % 2, :], ACT.Copy).then_inc(mer_hi_done, 1)

            def tanh_gate(q):
                act.wait_ge(gate_step, GATE_OPS * q + GATE_OPS)
                act.activation(tanh_gap[:], half_gap[:], ACT.Tanh).then_inc(tanh_done, 1)

            def copy_gate(q, first):
                act.wait_ge(cw_turned, q + 1)
                if not first:
                    act.wait_ge(cw_stored, 16 * q)
                act.activation(cw_row[:], bank[0:EXPERTS * BLOCKS, GATE, P:2 * P], ACT.Copy, scale=0.5)\
                   .then_inc(cw_copied, 1)

            def hidden(n, s, first=False):
                e = s % EXPERTS
                for f in range(FC):
                    if f % 2 == 0 and not first:
                        act.wait_ge(lo_done, 2 * n + f // 2 - 1)
                    act.wait_ge(h_done, FC * n + f + 1)
                    act.activation(act_out[:, f // 2, f % 2, :], bank[:, f, :], ACT.Gelu_apprx_tanh,
                                   bias=vec[:, V_B1 + e * FC + f:V_B1 + e * FC + f + 1]).then_inc(g_done, 1)
                    if f % 2 == 1:
                        if f == 1:
                            act.wait_ge(y_done, Y_COND if first else n + Y_COND - 1)
                        act.wait_ge(g_done, FC * n + f + 1)
                        act.activation(hid_hi[:, s % 2, f - 1:f + 1, :], act_out[:, f // 2, :, :], ACT.Copy)\
                           .then_inc(hi_done, 1)

            def project_high(c):
                act.wait_ge(proj_done, c + 1)
                for j in range(PER_CHUNK):
                    b, t = PER_CHUNK * c + j, slice(j * SEQ, (j + 1) * SEQ)
                    act.activation(xhi[:, c, t], bank[:, project_bank(c), t], ACT.Identity, bias=emb[:, b:b + 1])\
                       .then_inc(z_hi, 1)

            def round_steps(rnd, last):
                for s in range(STEPS):
                    n = STEPS * rnd + s
                    if s <= EXPERTS:
                        if s % EXPERTS == 0:
                            copy_gate(CHUNKS * rnd + CHUNKS - 2 + s // EXPERTS, False)
                    elif s % EXPERTS == 0 and not last:
                        copy_gate(CHUNKS * (rnd + 1) + s // EXPERTS - 2, False)
                    if s < STEPS - 1:
                        hidden(n + 1, s + 1)
                    elif not last:
                        hidden(n + 1, 0)
                    c = s // EXPERTS - 1
                    if s == 2:
                        tanh_gate(CHUNKS * rnd + CHUNKS - 1)
                    elif s % EXPERTS == 1 and s > 1 and last:
                        project_high(c)
                    elif s % EXPERTS == 2 and not last:
                        tanh_gate(CHUNKS * (rnd + 1) + c)
                    if last and s < FFN_PIECES:
                        act.wait_ge(ffn_in[s // RING], 16)
                        act.activation(ffn_hi[:, s, :], ffn_raw[:, s % RING, :], ACT.Copy).then_inc(ffn_hi_done, 1)

            def relu_high(b):
                act.wait_ge(cond_h_done, b + 1)
                if b >= 2:
                    act.wait_ge(y_done, b - 1)
                act.activation(hid_hi[:, b % 2, 0:2, :], bank[:, 2 * (b % 2):2 * (b % 2) + 2, :], ACT.Relu)\
                   .then_inc(relu_hi, 1)

            def conditioned(c):
                act.wait_ge(y_done, PER_CHUNK * (c + 1))
                if c >= CHUNKS - 2:
                    act.wait_ge(merge_free, 2 * BATCHES)
                act.activation(cur[:, c, :], bank[:, 4 + c % 2, :], ACT.Copy).then_inc(cond_cur, 1)
                act.activation(xhi[:, c, :], bank[:, 4 + c % 2, :], ACT.Copy).then_inc(cond_xhi, 1)

            act.wait_ge(const_done, 2 + EXPERTS)
            act.activation(low_any[0:1, :], need[0:1, 0:1], ACT.Gelu_apprx_tanh)
            for m in range(EARLY - 1):
                merged_high(m)
            for i in range(4):
                half = slice((i % 2) * 2 * F, (i % 2 + 1) * 2 * F)
                act.dma_start(moe_raw[:, i // 2, half], moe_w[:, i // 2, half]).then_inc(moe_in[i], 16)
            relu_high(0)
            for b in range(BATCHES):
                c = b // 2 - 1
                if b % 2 == 0 and c >= 0:
                    conditioned(c)
                if 2 * b + 5 < MERGES:
                    merged_high(2 * b + 5)
                if b % 2 == 0 and c + 2 < CHUNKS:
                    act.wait_ge(x_in[c + 2], 16)
                    act.activation(xhi[:, c + 2, :], x0[:, c + 2, :], ACT.Copy).then_inc(x0_hi, 1)
                if b + 1 < BATCHES:
                    relu_high(b + 1)
                if b % 2 == 0 and c >= 1:
                    copy_gate(c - 1, c == 1)
                if 2 * b + 6 < MERGES:
                    merged_high(2 * b + 6)
                for i in MOE_AT.get(b, ()):
                    piece = slice((i % EXPERTS) * F, (i % EXPERTS + 1) * F)
                    act.wait_ge(moe_in[i // 2], 16)
                    act.activation(moe_hi[:, i // EXPERTS, piece], moe_raw[:, i // EXPERTS, piece], ACT.Copy)\
                       .then_inc(moe_hi_done, 1)
                if b % 2 == 1 and b >= 3:
                    tanh_gate(c)

            conditioned(CHUNKS - 1)
            act.wait_ge(mer_lo_done, 2 * BATCHES)
            hidden(0, 0, True)
            with act.Fori(0, ROUNDS - 1) as rnd:
                round_steps(rnd, False)
            round_steps(ROUNDS - 1, True)

            def high(t, pr, done, count):
                if pr == 0:
                    if t < 2:
                        act.wait_ge(y_done, Y_MOE - 1 + t)
                    elif t > 2:
                        stage, c = [x for x in FFN_ORDER if 1 <= x[0] <= 3][t - 3]
                        if stage < 3:
                            act.wait_ge(o_done, FC * wide_at(stage + 1, c) + FC)
                        else:
                            act.wait_ge(y_done, Y_MOE + c + 1)
                act.wait_ge(done, count)
                act.activation(hid_hi[:, t % 3, 2 * pr:2 * pr + 2, :], act_out[:, pr, :, :], ACT.Copy)\
                   .then_inc(hi_done, 1)

            for stage, c in FFN_ORDER:
                if stage == 0:
                    project_high(c)
                elif stage == 1:
                    for f in range(FC):
                        act.wait_ge(gated_done, FC * c + f + 1)
                        act.wait_ge(add_done, ADD_MOE + FC * c + f - 1)
                        act.activation(prod[:, f % 2, :], bank[:, 2 * f, :], ACT.Silu,
                                       scale=vec[:, V_S1 + f:V_S1 + f + 1]).then_inc(silu_done, 1)
                        if f >= 2:
                            high(split_at(1, c), f - 2, add_done, ADD_MOE + FC * c + 2 * (f - 2) + 2)
                elif stage < 4:
                    t, at, v = split_at(stage, c), FC * wide_at(stage, c), V_H1 if stage == 2 else V_H2
                    for o in range(FC):
                        act.wait_ge(o_done, at + o + 1)
                        if o % 2 == 0:
                            act.wait_ge(lo_done, LO_MOE + 2 * t + o // 2 - 1)
                        act.activation(act_out[:, o // 2, o % 2, :], bank[:, o + 4 * (c % 2), :], ACT.Gelu,
                                       scale=vec[:, v + o:v + o + 1]).then_inc(gelu_done, 1)
                        if o % 2 == 1:
                            high(t, o // 2, gelu_done, at + o + 1)

        @block.vector
        def _(dve):
            def x0_low(c):
                dve.wait_ge(x0_hi, c + 1)
                dve.tensor_tensor(xlo[:, c, :], x0[:, c, :], xhi[:, c, :].bitcast(F32), ALU.subtract)\
                   .then_inc(x0_split, 1)

            def merged_sum(m):
                if m >= 2 * BATCHES:
                    half = m - 2 * BATCHES
                    dve.wait_ge(mer_hi_done, m + 1)
                    pick = slice(4 * half, 4 * half + 4)
                    dve.tensor_tensor(lang_lo[:, pick, :].rearrange("p b d -> p (b d)"), bank[:, MERGE, :],
                                      lang_hi[:, pick, :].rearrange("p b d -> p (b d)").bitcast(F32),
                                      ALU.subtract).then_inc(merge_free, 1)
                    return
                b = m // 2
                if m == 0:
                    dve.wait_ge(base_in, 16)
                dve.wait_ge(merge_done, m + 1)
                if m >= 2:
                    dve.wait_ge(mer_lo_done, m - 1)
                dve.scalar_tensor_tensor(merged[:, m % 2, :], bank[:, merge_bank(m), :], COND_ALPHA, base[:, m % 2, :],
                                         ALU.mult, ALU.add).then_inc(merge_free, 1)

            def gate_scores(c, rnd):
                q = CHUNKS * rnd + c
                at = GATE_OPS * q
                shape = [P, BLOCKS, EXPERTS, EXPERTS]
                dve.wait_ge(logit_done, q + 1)
                dve.tensor_tensor(logit[:], bank[:, GATE, 0:BLOCKS * EXPERTS].rearrange("p (t e) -> p t e", e=EXPERTS),
                                  gbias[:, bass.ds(EXPERTS * rnd, EXPERTS)].unsqueeze(1)
                                  .to_broadcast([P, BLOCKS, EXPERTS]), ALU.add).then_inc(gate_step, 1)
                dve.wait_ge(gate_step, at + 1)
                dve.tensor_tensor(beats[:], logit[:].unsqueeze(3).to_broadcast(shape),
                                  logit[:].unsqueeze(2).to_broadcast(shape), ALU.is_ge).then_inc(gate_step, 1)
                dve.tensor_reduce(top[:], logit[:], AX_X, ALU.max).then_inc(gate_step, 1)
                dve.wait_ge(gate_step, at + 2)
                dve.tensor_tensor(beats_up[:].rearrange("p t i j -> p t (i j)"),
                                  beats[:].rearrange("p t i j -> p t (i j)"),
                                  upper[:].rearrange("p i j -> p (i j)").unsqueeze(1)
                                  .to_broadcast([P, BLOCKS, EXPERTS * EXPERTS]), ALU.mult).then_inc(gate_step, 1)
                dve.wait_ge(gate_step, at + 3)
                dve.tensor_tensor(below[:], logit[:], top[:].unsqueeze(2).to_broadcast([P, BLOCKS, EXPERTS]),
                                  ALU.subtract).then_inc(gate_step, 1)
                dve.wait_ge(gate_step, at + 4)
                dve.tensor_tensor(net[:], beats_up[:], beats_up[:].rearrange("p t i j -> p t j i"),
                                  ALU.subtract).then_inc(gate_step, 1)
                dve.wait_ge(gate_step, at + 6)
                dve.tensor_reduce(wins[:], net[:], AX_X, ALU.add).then_inc(gate_step, 1)
                dve.wait_ge(gate_step, at + 7)
                dve.tensor_tensor(chosen[:], wins[:], need[:].unsqueeze(1).to_broadcast([P, BLOCKS, EXPERTS]),
                                  ALU.is_ge).then_inc(gate_step, 1)
                dve.wait_ge(gate_step, at + 8)
                dve.tensor_tensor(below_ch[:], below[:], chosen[:], ALU.mult).then_inc(gate_step, 1)
                dve.wait_ge(gate_step, at + 9)
                dve.tensor_reduce(second[:], below_ch[:], AX_X, ALU.add).then_inc(gate_step, 1)
                dve.wait_ge(gate_step, at + 10)
                dve.scalar_tensor_tensor(half_gap[:], second[:].unsqueeze(2).to_broadcast([P, BLOCKS, EXPERTS]),
                                         -0.5, below[:], ALU.mult, ALU.add).then_inc(gate_step, 1)

            def gate_weights(q):
                dve.wait_ge(tanh_done, q + 1)
                dve.scalar_tensor_tensor(cw_tok[:].rearrange("p e t -> p t e"), tanh_gap[:], 1.0, chosen[:],
                                         ALU.add, ALU.mult).then_inc(cw_done, 1)

            def hidden_low(n, s):
                for pr in range(2):
                    dve.wait_ge(hi_done, 2 * n + pr + 1)
                    dve.tensor_tensor(hid_lo[:, s % 2, 2 * pr:2 * pr + 2, :], act_out[:, pr, :, :],
                                      hid_hi[:, s % 2, 2 * pr:2 * pr + 2, :].bitcast(F32), ALU.subtract)\
                       .then_inc(lo_done, 1)

            def round_steps(rnd, last):
                for s in range(STEPS):
                    n, c, e = STEPS * rnd + s, s // EXPERTS, s % EXPERTS
                    if s == 3:
                        gate_weights(CHUNKS * rnd + CHUNKS - 1)
                    elif s % EXPERTS == 3 and not last:
                        gate_weights(CHUNKS * (rnd + 1) + c - 1)
                    if s < STEPS - 1:
                        hidden_low(n + 1, s + 1)
                    elif not last:
                        hidden_low(n + 1, 0)
                    if last and e == 1 and c >= 1:
                        project_low(c - 1)
                    if e == 0:
                        dve.wait_ge(cw_ready[c % 2], 16 * (2 * rnd + c // 2 + 1))
                    dve.wait_ge(y_done, Y_COND + n + 1)
                    dve.wait_ge(add_done, n + 1)
                    dve.scalar_tensor_tensor(prod[:, s % 2, :], bank[:, 4 + s % 2, :], vec[:, V_B2 + e:V_B2 + e + 1],
                                             cw_all[:, c % 2, e, :], ALU.add, ALU.mult).then_inc(prod_done, 1)
                    dve.wait_ge(prod_done, n + 1)
                    dve.wait_ge(add_done, ADD0 + n)
                    dve.tensor_tensor(cur[:, c, :], cur[:, c, :], prod[:, s % 2, :], ALU.add).then_inc(add_done, 1)
                    if s == 1:
                        gate_scores(CHUNKS - 1, rnd)
                    elif s % EXPERTS == 1 and not last:
                        gate_scores(c - 1, rnd + 1)
                    if last and 1 <= s <= FFN_PIECES:
                        dve.wait_ge(ffn_lo_done, s)
                        dve.tensor_reduce(low_max[:, s - 1:s], ffn_lo[:, s - 1, :].bitcast(F32), AX_X, ALU.max,
                                          apply_absolute_value=True).then_inc(low_max_done, 1)
                    elif last and s == FFN_PIECES + 1:
                        dve.wait_ge(low_max_done, FFN_PIECES)
                        dve.tensor_reduce(low_row[:], low_max[:], AX_X, ALU.max).then_inc(low_max_done, 1)
                    if e == EXPERTS - 1 and not (last and s == STEPS - 1):
                        split_cur(rnd, c, last)

            def split_cur(rnd, c, last):
                dve.wait_ge(add_done, ADD0 + STEPS * rnd + EXPERTS * c + EXPERTS)
                if last:
                    dve.tensor_tensor(cur[:, c, :], cur[:, c, :], x0[:, c, :], ALU.add).then_inc(res_done, 1)
                    dve.wait_ge(res_done, c + 1)
                dve.tensor_copy(xhi[:, c, :], cur[:, c, :]).then_inc(xhi_done, 1)
                dve.wait_ge(xhi_done, CHUNKS * rnd + c + 1)
                dve.tensor_tensor(xlo[:, c, :], cur[:, c, :], xhi[:, c, :].bitcast(F32), ALU.subtract)\
                   .then_inc(xs_done, 1)

            def project_low(c):
                dve.wait_ge(z_hi, PER_CHUNK * c + PER_CHUNK)
                for j in range(PER_CHUNK):
                    b, t = PER_CHUNK * c + j, slice(j * SEQ, (j + 1) * SEQ)
                    dve.scalar_tensor_tensor(xlo[:, c, t], bank[:, project_bank(c), t], emb[:, b:b + 1],
                                             xhi[:, c, t].bitcast(F32), ALU.add, ALU.subtract).then_inc(evac_done, 1)

            def conditioned_low(c):
                dve.wait_ge(cond_cur, c + 1)
                dve.wait_ge(cond_xhi, c + 1)
                dve.tensor_tensor(xlo[:, c, :], bank[:, 4 + c % 2, :], xhi[:, c, :].bitcast(F32), ALU.subtract)\
                   .then_inc(xs_done, 1)

            def relu_low(b):
                dve.wait_ge(relu_hi, b + 1)
                dve.scalar_tensor_tensor(hid_lo[:, b % 2, 0:2, :], bank[:, 2 * (b % 2):2 * (b % 2) + 2, :], 0.0,
                                         hid_hi[:, b % 2, 0:2, :].bitcast(F32), ALU.max, ALU.subtract)\
                   .then_inc(relu_lo, 1)

            dve.wait_ge(x_in[0], 16)
            dve.tensor_copy(xhi[:, 0, :], x0[:, 0, :]).then_inc(x0_hi, 1)
            x0_low(0)
            for m in range(EARLY - 1):
                merged_sum(m)
            relu_low(0)
            for b in range(BATCHES):
                c = b // 2 - 1
                if 2 * b + 5 < MERGES:
                    merged_sum(2 * b + 5)
                if b % 2 == 1 and c >= 0:
                    if c == 0:
                        dve.wait_ge(small_in, 32)
                        dve.wait_ge(const_done, 4 + EXPERTS)
                    gate_scores(c, 0)
                if 2 * b + 6 < MERGES:
                    merged_sum(2 * b + 6)
                if b + 1 < BATCHES:
                    relu_low(b + 1)
                if b % 2 == 1 and c >= 0:
                    gate_weights(c)
                if b % 2 == 0:
                    if c >= 0:
                        conditioned_low(c)
                    if c + 2 < CHUNKS:
                        x0_low(c + 2)
            conditioned_low(CHUNKS - 1)
            dve.wait_ge(xs_done, CHUNKS)
            for i in range(2):
                dve.memset(prod[:, i, :], 0.0).then_inc(add_done, 1)

            hidden_low(0, 0)
            with dve.Fori(0, ROUNDS - 1) as rnd:
                round_steps(rnd, False)
            round_steps(ROUNDS - 1, True)

            for stage, c in FFN_ORDER:
                if stage == 0:
                    project_low(c)
                    continue
                if stage < 4:
                    t = split_at(stage, c)
                for i in range(FC):
                    if stage == 1:
                        dve.wait_ge(silu_done, FC * c + i + 1)
                        dve.wait_ge(lo_done, LO_MOE + 2 * t + i // 2 - 1)
                        dve.scalar_tensor_tensor(act_out[:, i // 2, i % 2, :], bank[:, 2 * i + 1, :],
                                                 vec[:, V_S2 + i:V_S2 + i + 1], prod[:, i % 2, :],
                                                 ALU.mult, ALU.mult).then_inc(add_done, 1)
                    if stage < 4 and i >= 2:
                        pr = i - 2
                        dve.wait_ge(hi_done, LO_MOE + 2 * t + pr + 1)
                        dve.tensor_tensor(hid_lo[:, t % 3, 2 * pr:2 * pr + 2, :], act_out[:, pr, :, :],
                                          hid_hi[:, t % 3, 2 * pr:2 * pr + 2, :].bitcast(F32), ALU.subtract)\
                           .then_inc(lo_done, 1)
                if stage == 1 and c == 0:
                    split_cur(ROUNDS - 1, CHUNKS - 1, True)
                if stage == 4:
                    dve.wait_ge(y_done, Y_MOE + c + 1)
                    dve.scalar_tensor_tensor(x0[:, c, :], bank[:, out_bank(c), :], vec[:, V_S3:V_S3 + 1], cur[:, c, :],
                                             ALU.mult, ALU.add).then_inc(evac_done, 1)


def kernel(**inputs):
    import numpy as np
    import concourse.bacc as bacc
    from concourse.bass_utils import run_bass_kernel_spmd

    a = {k: np.asarray(v) for k, v in inputs.items()}

    def down(w):
        return w.T.reshape(-1, P, w.shape[0]).transpose(1, 0, 2)

    def cols(v):
        return v.reshape(-1, P).T

    def factors(ia, ib, oa, ob):
        return np.concatenate([ia, np.swapaxes(ib, -1, -2), oa, np.swapaxes(ob, -1, -2)], axis=-1)

    c, f, g = "L0_cond_", "L0_ffn_", "L1_ffn_"
    common, expert = (factors(*(a[f"{c}{kind}_{w}"] for w in ("wi_a", "wi_b", "wo_a", "wo_b")))
                      for kind in ("common", "experts"))
    arrays = {
        "x_t": a["x"].reshape(TOKENS, D).T,
        "batch_ids": np.concatenate([a["itok_B_0_7"], a["itok_B_0_3"]]).reshape(1, 2 * BATCHES),
        "cond_base": np.stack([a[c + "wi"].T, down(a[c + "wo"]).reshape(P, F)], axis=1),
        "lora_all": np.concatenate([np.broadcast_to(common, expert.shape), expert], axis=1),
        "lang_lora": np.concatenate([a["L1_cond_lora_A"], np.swapaxes(a["L1_cond_lora_B"], 1, 2)], axis=2),
        "lang_embed": a["L1_cond_lang_embed"],
        "moe_w": np.stack([a[f + "W1"].transpose(1, 0, 2).reshape(P, EXPERTS * F),
                           a[f + "W2"].reshape(EXPERTS * FC, P, D).transpose(1, 0, 2).reshape(P, EXPERTS * F)], axis=1),
        "vecs": np.concatenate([cols(a[f + "b1"]), cols(a[f + "b2"]), cols(a[g + "w1_s"]), cols(a[g + "w2_s"]),
                                cols(a[g + "h1_s"]), cols(a[g + "h2_s"]), cols(a[g + "w3_s"]),
                                a[f + "Wg"].transpose(1, 0, 2).reshape(P, ROUNDS * EXPERTS)], axis=1),
        "gate_bias": a[f + "bg"].reshape(1, ROUNDS * EXPERTS),
        "ffn_w": np.concatenate([a[g + "w1_w"].T[:, None, :], a[g + "w2_w"].T[:, None, :], down(a[g + "h1_w"]),
                                 down(a[g + "h2_w"]), down(a[g + "w3_w"]).reshape(P, 1, F)], axis=1),
    }
    arrays = {k: np.ascontiguousarray(v) for k, v in arrays.items()}
    nc = bacc.Bacc("TRN2", target_bir_lowering=False, num_devices=1)
    args = [nc.dram_tensor(k, v.shape, mybir.dt.from_np(v.dtype), kind="ExternalInput").ap()
            for k, v in arrays.items()]
    out = nc.dram_tensor("out_t", (P, TOKENS), F32, kind="ExternalOutput").ap()
    adaln_ffn(nc, *args, out)
    r = run_bass_kernel_spmd(nc, [arrays], core_ids=[0])
    return np.ascontiguousarray(r.results[0]["out_t"].T).reshape(BATCHES, SEQ, D)
```

```python
from contextlib import ExitStack

import concourse.bass as bass
from concourse import mybir

ACT = mybir.ActivationFunctionType
ALU = mybir.AluOpType
AX_X = mybir.AxisListType.X
F32 = mybir.dt.float32
F32R = mybir.dt.float32r
I32 = mybir.dt.int32

P = 128
BATCHES, SEQ, D = 8, 256, 128
TOKENS = BATCHES * SEQ
CHUNK = 512
CHUNKS = TOKENS // CHUNK
PER_CHUNK = CHUNK // SEQ
F = 512
FC = F // P
RANK = 16
LORA_EXPERTS, LANGS = 8, 4
COND_ALPHA = 2.0
EXPERTS, ROUNDS = 4, 4
STEPS = CHUNKS * EXPERTS
SQ = 32
BLOCKS = CHUNK // SQ
LORA_W = D + F + F + D
FFN_PIECES = 3 + 2 * FC
RING = 6
MOE_PIECES = 2 * EXPERTS

MERGES = 2 * BATCHES + 2
EARLY = 6
AHEAD = 4
AFTER_GATE = (13, 17)
LOAD_AFTER = [0, 1, 3, 4]
MOE_AT = {0: [0], 1: [1], 2: [2], 3: [3], 5: [4, 5], 6: [6, 7]}
WARM, KEEP_WARM = 12, 2

V_B1, V_B2, V_S1, V_S2, V_H1, V_H2, V_S3, V_WG = 0, 16, 20, 24, 28, 32, 36, 37
V_N = V_WG + ROUNDS * EXPERTS

Y_COND = BATCHES
Y_MOE = Y_COND + ROUNDS * STEPS
ADD0 = 2
LO_MOE = 2 * ROUNDS * STEPS
Z_ALL = 2 * CHUNKS
CONSTS = 5 + EXPERTS
GATE_OPS = 14
GATE_HALF = 8

GATED, H1, H2, W3, PROJECT, MIXTURE = range(6)
FFN_UNITS = ([(GATED, 0, 0), (GATED, 0, 1), (MIXTURE, CHUNKS - 1, 0), (GATED, 0, 2), (GATED, 0, 3)]
             + [(GATED, c, f) for c in range(1, CHUNKS - 1) for f in range(FC)]
             + [(H1, 0, 0), (PROJECT, CHUNKS - 1, 0), (H1, 0, 1), (GATED, CHUNKS - 1, 0), (GATED, CHUNKS - 1, 1),
                (H1, 0, 2), (GATED, CHUNKS - 1, 2), (GATED, CHUNKS - 1, 3), (H1, 0, 3)]
             + [(H1, c, o) for c in range(1, CHUNKS) for o in range(FC)]
             + [(H2, 0, o) for o in range(FC)]
             + [u for c in range(1, CHUNKS) for u in [(H2, c, o) for o in range(FC)] + [(W3, c - 1, 0)]]
             + [(W3, CHUNKS - 1, 0)])
FFN_STAGES = ([(GATED, c) for c in range(CHUNKS - 1)] + [(PROJECT, CHUNKS - 1), (GATED, CHUNKS - 1)]
              + [(H1, c) for c in range(CHUNKS)] + [(H2, 0)]
              + [u for c in range(1, CHUNKS) for u in [(H2, c), (W3, c - 1)]] + [(W3, CHUNKS - 1)])
LAST_STAGE = (H2, CHUNKS - 1)
SLOTS = 5


def hidden_at(kind, c):
    return CHUNKS * kind + c


def wide_at(kind, c):
    return CHUNKS * (kind - H1) + c


def adaln_ffn(nc, x_t, batch_ids, cond_base, lora_all, lang_lora, lang_embed,
              moe_w, vecs, gate_bias, ffn_w, out_t):
    ctx = ExitStack()
    with ctx:
        def sb(name, shape, dt):
            return ctx.enter_context(nc.sbuf_tensor(name, shape, dt))

        def sem(name):
            return ctx.enter_context(nc.semaphore(name))

        x0 = sb("x0", [P, CHUNKS, CHUNK], F32)
        cur = sb("cur", [P, CHUNKS, CHUNK], F32)
        xhi = sb("xhi", [P, CHUNKS, CHUNK], F32R)
        xlo = sb("xlo", [P, CHUNKS, CHUNK], F32R)
        moe_hi = sb("moe_hi", [P, 2, EXPERTS * F], F32R)
        moe_lo = sb("moe_lo", [P, 2, EXPERTS * F], F32R)
        ffn_hi = sb("ffn_hi", [P, FFN_PIECES, F], F32R)
        ffn_lo = sb("ffn_lo", [P, FFN_PIECES, F], F32R)
        lang_hi = sb("lang_hi", [P, BATCHES, D], F32R)
        lang_lo = sb("lang_lo", [P, BATCHES, D], F32R)
        hid_hi = sb("hid_hi", [P, 2, FC, CHUNK], F32R)
        hid_lo = sb("hid_lo", [P, 2, FC, CHUNK], F32R)
        act_out = sb("act_out", [P, 2, 2, CHUNK], F32)
        cw_all = sb("cw_all", [P, 2, EXPERTS, CHUNK], F32)
        prod = sb("prod", [P, 2, CHUNK], F32)
        stage = sb("stage", [P, RING * F], F32)
        vec = sb("vec", [P, V_N], F32)
        low_max = sb("low_max", [P, FFN_PIECES], F32)
        low_row = sb("low_row", [P, 1], F32)
        low_any = sb("low_any", [P, 1], F32)
        emb = sb("emb", [P, BATCHES], F32)
        gbias = sb("gbias", [SQ, ROUNDS * EXPERTS], F32)
        wg_raw = sb("wg_raw", [P, ROUNDS, SQ], F32)
        wg = sb("wg", [P, ROUNDS, SQ], F32R)
        wg_now = sb("wg_now", [P, SQ], F32R)
        ids = sb("ids", [1, 2 * BATCHES], I32)
        blank = sb("blank", [P, P], F32)
        upper = sb("upper", [SQ, EXPERTS, EXPERTS], F32)
        need = sb("need", [SQ, EXPERTS], F32)
        turned = sb("turned", [SQ, BLOCKS, SQ], F32)
        logit_lo = sb("logit_lo", [SQ, BLOCKS, EXPERTS], F32)
        logit = sb("logit", [SQ, BLOCKS, EXPERTS], F32)
        beats = sb("beats", [SQ, BLOCKS, EXPERTS, EXPERTS], F32)
        beats_up = sb("beats_up", [SQ, BLOCKS, EXPERTS, EXPERTS], F32)
        net = sb("net", [SQ, BLOCKS, EXPERTS, EXPERTS], F32)
        wins = sb("wins", [SQ, BLOCKS, EXPERTS], F32)
        chosen = sb("chosen", [SQ, BLOCKS, EXPERTS], F32)
        half_chosen = sb("half_chosen", [SQ, BLOCKS, EXPERTS], F32)
        top = sb("top", [SQ, BLOCKS], F32)
        below = sb("below", [SQ, BLOCKS, EXPERTS], F32)
        below_ch = sb("below_ch", [SQ, BLOCKS, EXPERTS], F32)
        second = sb("second", [SQ, BLOCKS], F32)
        half_gap = sb("half_gap", [SQ, BLOCKS, EXPERTS], F32)
        tanh_gap = sb("tanh_gap", [SQ, BLOCKS, EXPERTS], F32)
        cw_tok = sb("cw_tok", [SQ, BLOCKS, SQ], F32)
        cw_row = sb("cw_row", [SQ, CHUNK], F32)
        cw_dram = nc.dram_tensor("cw_dram", [2, EXPERTS * CHUNK], F32).ap()

        base = cur[:, CHUNKS - 2:CHUNKS, :]
        lora = stage[:, 0:2 * LORA_W].rearrange("p (h n) -> p h n", h=2)
        lang_f = [at.rearrange("p h (b n) -> p (h b) n", n=2 * D) for at in (act_out[:, 0, :, :], prod[:])]
        mer_hi = ffn_hi[:, 0:2 * AHEAD, :].rearrange("p (b m) f -> p b m f", m=2)
        mer_lo = ffn_lo[:, 0:2 * AHEAD, :].rearrange("p (b m) f -> p b m f", m=2)
        moe_raw = cw_all[:].rearrange("p s e t -> p s (e t)")
        silu = stage[:, 0:FC * CHUNK].rearrange("p (f t) -> p f t", t=CHUNK)
        ffn_raw = stage[:].rearrange("p (i f) -> p i f", f=F)

        bank = ctx.enter_context(nc.psum_tensor("bank", [P, 8, CHUNK], F32))
        MERGE, GATE, LAST = 6, 7, 3

        x_in = [sem(f"x_in{c}") for c in range(CHUNKS)]
        ids_in, base_in, lang_in, small_in = (sem(n) for n in ("ids_in", "base_in", "lang_in", "small_in"))
        lora_in = [sem(f"lora_in{b}") for b in range(BATCHES)]
        moe_in = [sem(f"moe_in{i}") for i in range(4)]
        ffn_in = [sem(f"ffn_in{i}") for i in range(1 + FFN_PIECES - RING)]
        const_done = sem("const_done")
        x0_hi, x0_split = sem("x0_hi"), sem("x0_split")
        merge_done = sem("merge_done")
        merge_free = sem("merge_free")
        mer_hi_done, mer_lo_done = sem("mer_hi_done"), sem("mer_lo_done")
        moe_hi_done, moe_lo_done = sem("moe_hi_done"), sem("moe_lo_done")
        cond_h_done = sem("cond_h_done")
        relu_hi, relu_lo = sem("relu_hi"), sem("relu_lo")
        cond_cur, cond_xhi = sem("cond_cur"), sem("cond_xhi")
        h_done = sem("h_done")
        g_done = sem("g_done")
        hi_done, lo_done = sem("hi_done"), sem("lo_done")
        y_done = sem("y_done")
        prod_done = sem("prod_done")
        add_done = sem("add_done")
        res_done = sem("res_done")
        xhi_done, xs_done = sem("xhi_done"), sem("xs_done")
        logit_done = sem("logit_done")
        gate_step, tanh_done = sem("gate_step"), sem("tanh_done")
        wg_step, wg_done = sem("wg_step"), sem("wg_done")
        cw_done, cw_turned, cw_stored = (sem(n) for n in ("cw_done", "cw_turned", "cw_stored"))
        cw_ready = [sem(f"cw_ready{i}") for i in range(2)]
        ffn_hi_done, ffn_lo_done = sem("ffn_hi_done"), sem("ffn_lo_done")
        low_max_done, low_any_done = sem("low_max_done"), sem("low_any_done")
        proj_done, z_hi = sem("proj_done"), sem("z_hi")
        evac_done = sem("evac_done")
        gated_done, silu_done = sem("gated_done"), sem("silu_done")
        unit_done = sem("unit_done")
        o_done, gelu_done = sem("o_done"), sem("gelu_done")
        low_done = [sem(f"low_done{i}") for i in range(2)]
        out_done = sem("out_done")

        block = ctx.enter_context(nc.Block())

        def lora_rows(b):
            return slice(32 * (b % 4), 32 * (b % 4) + 2 * RANK)

        def merged(m):
            return cur[:, m - 2, :] if m in (2, 3) else act_out[:, 1, m % 2, :]

        def merge_bank(m):
            return GATE if m % 2 == 1 and (m < 2 * AHEAD + 2 or m in AFTER_GATE) else MERGE

        def merge_before(m):
            return max(k for k in range(m) if merge_bank(k) == merge_bank(m))

        def project_bank(c):
            return LAST if c == CHUNKS - 1 else GATE

        def gated_bank(c, f):
            return (0, 2, 6, 4)[f] if c < CHUNKS - 1 else FC + 2 * (f % 2)

        def out_bank(c):
            return FC - 1 + FC * (c % 2)

        def out_parts(c):
            parts = 2 if c == CHUNKS - 1 else 1
            return [slice(i * CHUNK // parts, (i + 1) * CHUNK // parts) for i in range(parts)]

        def unsplit(t):
            return cw_all[:, t % 2, :, :] if t < CHUNKS else act_out[:].rearrange("p a b t -> p (a b) t")

        def l1_hidden(hidden, mixture, x, t):
            if t % SLOTS < 2:
                return hidden[:, t % SLOTS, :, :]
            return x if t % SLOTS == 4 else mixture[:, t % SLOTS - 2, :].rearrange("p (i t) -> p i t", t=CHUNK)

        def l1_hi(t):
            return l1_hidden(hid_hi, moe_hi, xhi, t)

        def l1_lo(t):
            return l1_hidden(hid_lo, moe_lo, xlo, t)

        def batch_cols(b):
            return slice(SEQ * (b % PER_CHUNK), SEQ * (b % PER_CHUNK) + SEQ)

        @block.sync
        def _(sp):
            sp.dma_start(ids[:], batch_ids).then_inc(ids_in, 16)
            sp.dma_start(base, cond_base).then_inc(base_in, 16)
            sp.wait_ge(ids_in, 16)
            for b in range(BATCHES):
                e = sp.value_load(ids[0:1, b:b + 1], min_val=0, max_val=LORA_EXPERTS - 1)
                sp.dma_start(lora[lora_rows(b), b // 4, :],
                             lora_all[bass.ds(e, 1), :, :].rearrange("e r n -> (e r) n")).then_inc(lora_in[b], 16)
                if b in LOAD_AFTER:
                    c = LOAD_AFTER.index(b)
                    sp.dma_start(x0[:, c, :], x_t[:, c * CHUNK:(c + 1) * CHUNK]).then_inc(x_in[c], 16)
                if b == 2:
                    for i in range(4):
                        half = slice((i % 2) * 2 * F, (i % 2 + 1) * 2 * F)
                        sp.dma_start(moe_raw[:, i // 2, half], moe_w[:, i // 2, half]).then_inc(moe_in[i], 16)
            sp.dma_start(vec[:], vecs).then_inc(small_in, 16)
            sp.dma_start(gbias[:], gate_bias.to_broadcast([SQ, ROUNDS * EXPERTS])).then_inc(small_in, 16)
            for b in range(BATCHES):
                e = sp.value_load(ids[0:1, BATCHES + b:BATCHES + b + 1], min_val=0, max_val=LANGS - 1)
                sp.dma_start(lang_f[b // 4][0:RANK, b % 4, :],
                             lang_lora[bass.ds(e, 1), :, :].rearrange("e r n -> (e r) n")).then_inc(lang_in, 16)
                sp.dma_start(emb[:, b:b + 1],
                             lang_embed[bass.ds(e, 1), :].rearrange("e d -> d e")).then_inc(lang_in, 16)

            def store_gate(slot, turned, read, stored):
                sp.wait_ge(cw_turned, turned)
                if read is not None:
                    sp.wait_ge(cw_ready[slot], read)
                sp.dma_start(cw_dram[slot:slot + 1, :].rearrange("s (e t) -> (s e) t", t=CHUNK),
                             cw_row[0:EXPERTS, :])\
                  .then_inc(cw_stored, 16)
                sp.wait_ge(cw_stored, stored)

            def broadcast_gate(slot):
                sp.dma_start(cw_all[:, slot, :, :].rearrange("p e t -> p (e t)"),
                             cw_dram[slot:slot + 1, :].to_broadcast([P, EXPERTS * CHUNK])).then_inc(cw_ready[slot], 16)

            for slot in range(2):
                store_gate(slot, slot + 1, None, 16 * slot + 16)
            sp.wait_ge(moe_lo_done, MOE_PIECES)
            for slot in range(2):
                broadcast_gate(slot)
            with sp.Fori(1, ROUNDS * CHUNKS // 2) as pair:
                read = sp.to_reg(16 * pair)
                counts = [(sp.to_reg(2 * pair + slot + 1), sp.to_reg(32 * pair + 16 * slot + 16),
                           sp.to_reg(2 * EXPERTS * pair + EXPERTS * (slot - 1) + ADD0)) for slot in range(2)]
                for slot, (turned, stored, gated) in enumerate(counts):
                    store_gate(slot, turned, read, stored)
                    sp.wait_ge(add_done, gated)
                    broadcast_gate(slot)
            stored = 0
            for c in range(CHUNKS):
                for t in out_parts(c):
                    stored += 1
                    sp.wait_ge(evac_done, Z_ALL + stored)
                    sp.dma_start(out_t[:, c * CHUNK:(c + 1) * CHUNK][:, t], x0[:, c, t]).then_inc(out_done, 16)
            sp.wait_ge(out_done, 16 * stored)

        @block.gpsimd
        def _(pool):
            pool.memset(blank[:], 0.0).then_inc(const_done, 1)
            pool.memset(wg_raw[:], 0.0).then_inc(const_done, 1)
            pool.memset(cw_tok[:], 0.0).then_inc(const_done, 1)
            pool.memset(upper[:], 1.0).then_inc(const_done, 1)
            for i in range(EXPERTS):
                pool.memset(need[:, i:i + 1], 2.0 - i).then_inc(const_done, 1)
            pool.wait_ge(const_done, 4)
            pool.affine_select(out=upper[:], in_=upper[:], compare_op=ALU.is_gt, fill=0.0, base=0,
                               pattern=[[-1, EXPERTS], [1, EXPERTS]], channel_multiplier=0).then_inc(const_done, 1)

            def conditioned_low(c):
                pool.wait_ge(cond_cur, c + 1)
                pool.wait_ge(cond_xhi, c + 1)
                pool.tensor_tensor(xlo[:, c, :], cur[:, c, :], xhi[:, c, :].bitcast(F32), ALU.subtract)\
                    .then_inc(xs_done, 1)

            for b in range(-1, BATCHES):
                for m in range(2 * b + 5 if b >= 0 else 0, min(2 * b + 7, 2 * BATCHES)):
                    pool.wait_ge(mer_hi_done, m + 1)
                    pool.tensor_tensor(mer_lo[:, m // 2 % AHEAD, m % 2, :], merged(m),
                                       mer_hi[:, m // 2 % AHEAD, m % 2, :].bitcast(F32), ALU.subtract)\
                        .then_inc(mer_lo_done, 1)
                    if m == 2 * b + 5 and b % 2 == 0 and b >= 2:
                        conditioned_low(b // 2 - 1)
                if b == 6:
                    conditioned_low(CHUNKS - 2)
                for i in MOE_AT.get(b, ()):
                    piece = slice((i % EXPERTS) * F, (i % EXPERTS + 1) * F)
                    pool.wait_ge(moe_hi_done, i + 1)
                    pool.tensor_tensor(moe_lo[:, i // EXPERTS, piece], moe_raw[:, i // EXPERTS, piece],
                                       moe_hi[:, i // EXPERTS, piece].bitcast(F32), ALU.subtract)\
                        .then_inc(moe_lo_done, 1)

            def mixture_add(rnd, s, last):
                n, c, e = STEPS * rnd + s, s // EXPERTS, s % EXPERTS
                if e == EXPERTS - 1:
                    return
                pool.wait_ge(prod_done, n + 1)
                pool.wait_ge(add_done, ADD0 + n)
                if last and e == 0:
                    pool.tensor_tensor(cur[:, c, :], cur[:, c, :], x0[:, c, :], ALU.add).then_inc(res_done, 1)
                    pool.wait_ge(res_done, c + 1)
                pool.tensor_tensor(cur[:, c, :], cur[:, c, :], prod[:, s % 2, :], ALU.add).then_inc(add_done, 1)

            pool.wait_ge(merge_done, MERGES)
            pool.dma_start(ffn_raw, ffn_w[:, 0:RING, :]).then_inc(ffn_in[0], 16)
            for i in range(2):
                pool.wait_ge(cond_xhi, CHUNKS - 1 + i)
                pool.memset(prod[:, i, :], 0.0).then_inc(add_done, 1)
            conditioned_low(CHUNKS - 1)
            with pool.Fori(0, ROUNDS - 1) as rnd:
                for s in range(STEPS):
                    mixture_add(rnd, s, False)
            for s in range(STEPS):
                mixture_add(ROUNDS - 1, s, True)
                if s == FFN_PIECES + 1:
                    pool.wait_ge(low_max_done, FFN_PIECES + 1)
                    pool.partition_all_reduce(low_any[:], low_row[:], P, bass.bass_isa.ReduceOp.max)\
                        .then_inc(low_any_done, 1)
                if s >= FFN_PIECES:
                    continue
                pool.wait_ge(ffn_hi_done, s + 1)
                pool.tensor_tensor(ffn_lo[:, s, :], ffn_raw[:, s % RING, :], ffn_hi[:, s, :].bitcast(F32),
                                   ALU.subtract).then_inc(ffn_lo_done, 1)
                if s + RING < FFN_PIECES:
                    pool.wait_ge(ffn_lo_done, s + 1)
                    pool.dma_start(ffn_raw[:, s, :], ffn_w[:, s + RING, :]).then_inc(ffn_in[s + 1], 16)
            for c in range(CHUNKS):
                t = hidden_at(GATED, c)
                pool.wait_ge(hi_done, LO_MOE + 2 * t + 1)
                pool.tensor_tensor(l1_lo(t)[:, 0:2, :], unsplit(t)[:, 0:2, :],
                                   l1_hi(t)[:, 0:2, :].bitcast(F32), ALU.subtract)\
                    .then_inc(low_done[0], 1)
                if c == 0:
                    pool.wait_ge(xhi_done, CHUNKS * ROUNDS)
                    pool.tensor_tensor(xlo[:, CHUNKS - 1, :], cur[:, CHUNKS - 1, :],
                                       xhi[:, CHUNKS - 1, :].bitcast(F32), ALU.subtract).then_inc(xs_done, 1)

        @block.tensor
        def _(pe):
            def product(out, w_hi, w_lo, r_hi, r_lo, start, stop):
                pe.matmul(out, w_hi, r_hi, start=start, stop=False)
                mm = pe.matmul(out, w_hi, r_lo, start=False, stop=stop and w_lo is None)
                if w_lo is None:
                    return mm
                return pe.matmul(out, w_lo, r_hi, start=False, stop=stop)

            def merge(m):
                if m >= 2:
                    pe.wait_ge(merge_free, merge_before(m) + 1)
                if m in AFTER_GATE:
                    pe.wait_ge(gate_step, GATE_OPS * AFTER_GATE.index(m) + 1)
                if m >= 2 * BATCHES:
                    pe.wait_ge(lang_in, 32 * BATCHES)
                    for j in range(4):
                        factors = lang_f[m - 2 * BATCHES][0:RANK, j, :]
                        mm = pe.matmul(bank[:, merge_bank(m), j * D:(j + 1) * D], factors[:, 0:D], factors[:, D:2 * D],
                                       start=True, stop=True)
                    mm.then_inc(merge_done, 1)
                    return
                b, rows, half = m // 2, lora_rows(m // 2), m // 2 // 4
                pe.wait_ge(lora_in[b], 16)
                if m % 2 == 0:
                    pe.matmul(bank[:, merge_bank(m), :], lora[rows, half, 0:D], lora[rows, half, D:D + F],
                              start=True, stop=True).then_inc(merge_done, 1)
                else:
                    for fc in range(FC):
                        a = D + F + fc * P
                        mm = pe.matmul(bank[:, merge_bank(m), fc * D:(fc + 1) * D], lora[rows, half, a:a + P],
                                       lora[rows, half, D + 2 * F:LORA_W], start=True, stop=True)
                    mm.then_inc(merge_done, 1)

            def cond_hidden(b):
                pe.wait_ge(mer_lo_done, 2 * b + 1)
                pe.wait_ge(x0_split, b // PER_CHUNK + 1)
                if b >= 2:
                    pe.wait_ge(relu_lo, b - 1)
                cols = batch_cols(b)
                for f in range(FC):
                    w = slice(f * P, (f + 1) * P)
                    mm = product(bank[:, 2 * (b % 2) + f // 2, (f % 2) * SEQ:(f % 2 + 1) * SEQ],
                                 mer_hi[:, b % AHEAD, 0, w], mer_lo[:, b % AHEAD, 0, w],
                                 xhi[:, b // PER_CHUNK, cols], xlo[:, b // PER_CHUNK, cols], True, True)
                mm.then_inc(cond_h_done, 1)

            def cond_out(b):
                c = b // PER_CHUNK
                pe.wait_ge(mer_lo_done, 2 * b + 2)
                pe.wait_ge(relu_lo, b + 1)
                if c >= 2 and b % PER_CHUNK == 0:
                    pe.wait_ge(cond_xhi, c - 1)
                for fc in range(FC):
                    w = slice(fc * D, (fc + 1) * D)
                    r = slice((fc % 2) * SEQ, (fc % 2 + 1) * SEQ)
                    mm = product(bank[:, 4 + c % 2, batch_cols(b)], mer_hi[:, b % AHEAD, 1, w], mer_lo[:, b % AHEAD, 1, w],
                                 hid_hi[:, b % 2, fc // 2, r], hid_lo[:, b % 2, fc // 2, r], fc == 0, fc == FC - 1)
                mm.then_inc(y_done, 1)

            def warm(count):
                for i in range(count):
                    pe.matmul(bank[:, 4, 0:P], blank[:], blank[:], start=True, stop=True)

            def logits(c):
                pe.matmul(bank[0:SQ, GATE, :], wg_now[:], xhi[:, c, :], start=True, stop=False)
                pe.matmul(bank[0:SQ, GATE, :], wg_now[:], xlo[:, c, :], start=False, stop=True).then_inc(logit_done, 1)

            def expert_in(n, s, rnd, pieces=range(FC)):
                c, e = s // EXPERTS, s % EXPERTS
                if e == 0:
                    pe.wait_ge(xs_done, CHUNKS * rnd + c + 1)
                for f in pieces:
                    if s != 0 or not isinstance(rnd, int) or rnd:
                        pe.wait_ge(g_done, FC * n + f - 3)
                    w = slice(e * F + f * P, e * F + (f + 1) * P)
                    product(bank[:, f, :], moe_hi[:, 0, w], moe_lo[:, 0, w], xhi[:, c, :], xlo[:, c, :],
                            True, True).then_inc(h_done, 1)

            def expert_out(n, s):
                e = s % EXPERTS
                pe.wait_ge(add_done, n + 1)
                for fc in range(FC):
                    if fc % 2 == 0:
                        pe.wait_ge(lo_done, 2 * n + fc // 2 + 1)
                    w = slice(e * F + fc * D, e * F + (fc + 1) * D)
                    mm = product(bank[:, 4 + s % 2, :], moe_hi[:, 1, w], moe_lo[:, 1, w],
                                 hid_hi[:, s % 2, fc, :], hid_lo[:, s % 2, fc, :], fc == 0, fc == FC - 1)
                mm.then_inc(y_done, 1)

            def project(c):
                pe.wait_ge(xs_done, CHUNKS * ROUNDS + c + 1)
                if c == 0:
                    pe.wait_ge(gate_step, GATE_OPS * (CHUNKS * ROUNDS - 1) + 1)
                    pe.wait_ge(merge_free, MERGES)
                elif c < CHUNKS - 1:
                    pe.wait_ge(evac_done, 2 * c)
                else:
                    pe.wait_ge(unit_done, FC * (c - 1) + LAST // 2 + 1)
                for j in range(PER_CHUNK):
                    b, t = PER_CHUNK * c + j, slice(j * SEQ, (j + 1) * SEQ)
                    mm = product(bank[:, project_bank(c), t], lang_hi[:, b, :], lang_lo[:, b, :], xhi[:, c, t], xlo[:, c, t],
                                 True, True)
                mm.then_inc(proj_done, 1)

            def round_steps(rnd, last):
                for s in range(STEPS):
                    n = STEPS * rnd + s
                    if s < STEPS - 1:
                        expert_in(n + 1, s + 1, rnd)
                    elif not last:
                        expert_in(n + 1, 0, rnd + 1)
                    c = s // EXPERTS - 1
                    if s == 1:
                        pe.wait_ge(xs_done, CHUNKS * rnd + CHUNKS)
                        pe.wait_ge(gate_step, GATE_OPS * (CHUNKS * rnd + CHUNKS - 2) + 1)
                        logits(CHUNKS - 1)
                    elif s % EXPERTS == 1:
                        if last:
                            project(c)
                        else:
                            if c == 0:
                                pe.wait_ge(wg_done, rnd + 2)
                            pe.wait_ge(xs_done, CHUNKS * (rnd + 1) + c + 1)
                            pe.wait_ge(gate_step, GATE_OPS * (CHUNKS * (rnd + 1) + c - 1) + 1)
                            logits(c)
                    if last and s == STEPS - 1:
                        return
                    if last and s == STEPS - 2:
                        pe.wait_ge(low_any_done, 1)
                        pe.reg_load(inexact, low_any[0:1, 0:1].bitcast(I32))
                    expert_out(n, s)

            inexact = pe.alloc_register("inexact")
            pe.wait_ge(const_done, 1)
            warm(WARM)
            for m in range(4):
                merge(m)
                if m >= 1:
                    warm(KEEP_WARM)
            cond_hidden(0)
            for m in range(4, EARLY):
                merge(m)
            for b in range(BATCHES):
                c = b // 2 - 1
                if b + 1 < BATCHES:
                    cond_hidden(b + 1)
                if 2 * b + 6 < MERGES:
                    merge(2 * b + 6)
                if b == BATCHES - 1:
                    pe.wait_ge(moe_lo_done, 1)
                    pe.wait_ge(relu_lo, b)
                    expert_in(0, 0, 0, range(0, 2))
                cond_out(b)
                if 2 * b + 7 < MERGES:
                    merge(2 * b + 7)
                if b % 2 == 0 and c >= 0:
                    pe.wait_ge(merge_free, 2 * b + 6)
                    if c == 0:
                        pe.wait_ge(wg_done, 1)
                    else:
                        pe.wait_ge(gate_step, GATE_OPS * (c - 1) + 1)
                    pe.wait_ge(xs_done, c + 1)
                    logits(c)

            expert_in(0, 0, 0, range(2, FC))
            pe.wait_ge(moe_lo_done, MOE_PIECES)
            with pe.Fori(0, ROUNDS - 1) as rnd:
                round_steps(rnd, False)
            round_steps(ROUNDS - 1, True)


            def gated(c, f, w_lo):
                at = gated_bank(c, f)
                if c == 0:
                    if f == 0:
                        pe.wait_ge(evac_done, Z_ALL - 2)
                    if f < 2:
                        pe.wait_ge(g_done, FC * (ROUNDS * STEPS - 1) + 2 * f + 2)
                    elif f == 3:
                        pe.wait_ge(prod_done, ROUNDS * STEPS)
                elif c < CHUNKS - 1:
                    pe.wait_ge(unit_done, FC * (c - 1) + f + 1)
                else:
                    if f == 0:
                        pe.wait_ge(evac_done, Z_ALL)
                    pe.wait_ge(unit_done, FC * c if f == 0 else FC * c - 1 if f == 1 else FC * c + f - 1)
                w = slice(f * P, (f + 1) * P)
                product(bank[:, at, :], ffn_hi[:, 0, w], w_lo and ffn_lo[:, 0, w], xhi[:, c, :], xlo[:, c, :], True, True)
                product(bank[:, at + 1, :], ffn_hi[:, 1, w], w_lo and ffn_lo[:, 1, w], xhi[:, c, :], xlo[:, c, :],
                        True, True).then_inc(gated_done, 1)

            def contract(out, piece, w, t, w_lo):
                for i in range(FC):
                    if i % 2 == 0:
                        pe.wait_ge(low_done[i // 2], t + 1)
                    elif i == FC - 1 and t == hidden_at(*LAST_STAGE):
                        pe.wait_ge(low_done[1], t + 2)
                    at, cols = piece(i, w)
                    mm = product(out, ffn_hi[:, at, cols], w_lo and ffn_lo[:, at, cols],
                                 l1_hi(t)[:, i, :], l1_lo(t)[:, i, :], i == 0, i == FC - 1)
                return mm

            def wide(kind, c, o, w_lo):
                at = wide_at(kind, c)
                if at == 0:
                    pe.wait_ge(unit_done, FC * (CHUNKS - 2) + o // 2 + 1)
                    if o == LAST:
                        pe.wait_ge(evac_done, Z_ALL)
                elif at == 1:
                    pe.wait_ge(unit_done, FC * (CHUNKS - 1) + 2 + o // 2 + 1)
                else:
                    pe.wait_ge(gelu_done, FC * (at - 2) + o + 1)
                    if o == FC - 1 and kind == H2 and c >= 2:
                        pe.wait_ge(evac_done, Z_ALL + c - 1)
                first = 2 + FC * (kind - H1)
                contract(bank[:, o + FC * (at % 2), :], lambda i, w: (first + i, w), slice(o * P, (o + 1) * P),
                         hidden_at(kind - 1, c), w_lo).then_inc(o_done, 1)

            def narrow(c, w_lo):
                pe.wait_ge(gelu_done, FC * wide_at(H2, c) + FC)
                contract(bank[:, out_bank(c), :], lambda i, w: (FFN_PIECES - 1, slice(i * P, (i + 1) * P)), None,
                         hidden_at(H2, c), w_lo).then_inc(y_done, 1)

            def ffn(w_lo):
                for kind, c, i in FFN_UNITS:
                    if kind == PROJECT:
                        project(c)
                    elif kind == MIXTURE:
                        expert_out(ROUNDS * STEPS - 1, STEPS - 1)
                    elif kind == GATED:
                        gated(c, i, w_lo)
                    elif kind == W3:
                        narrow(c, w_lo)
                    else:
                        wide(kind, c, i, w_lo)

            with pe.If_eq(inexact, 0):
                ffn(None)
            with pe.Else():
                ffn(True)

        @block.scalar
        def _(act):
            def merged_high(m):
                if m >= 2 * BATCHES:
                    act.wait_ge(merge_done, m + 1)
                    half = m - 2 * BATCHES
                    act.activation(lang_hi[:, 4 * half:4 * half + 4, :].rearrange("p b d -> p (b d)"),
                                   bank[:, merge_bank(m), :], ACT.Copy).then_inc(mer_hi_done, 1)
                    return
                b = m // 2
                act.wait_ge(merge_free, m + 1)
                if b >= AHEAD:
                    act.wait_ge(cond_h_done if m % 2 == 0 else y_done, b - AHEAD + 1)
                act.activation(mer_hi[:, b % AHEAD, m % 2, :], merged(m), ACT.Copy).then_inc(mer_hi_done, 1)

            def tanh_gate(q):
                act.wait_ge(gate_step, GATE_OPS * q + GATE_OPS)
                act.activation(tanh_gap[:], half_gap[:], ACT.Tanh).then_inc(tanh_done, 1)

            def hidden(n, s, first=False):
                e = s % EXPERTS
                for f in range(FC):
                    if f % 2 == 0 and not first:
                        act.wait_ge(lo_done, 2 * n + f // 2 - 1)
                    act.wait_ge(h_done, FC * n + f + 1)
                    act.activation(act_out[:, f // 2, f % 2, :], bank[:, f, :], ACT.Gelu_apprx_tanh,
                                   bias=vec[:, V_B1 + e * FC + f:V_B1 + e * FC + f + 1]).then_inc(g_done, 1)
                    if f % 2 == 1:
                        if f == 1:
                            act.wait_ge(y_done, Y_COND if first else n + Y_COND - 1)
                        act.wait_ge(g_done, FC * n + f + 1)
                        act.activation(hid_hi[:, s % 2, f - 1:f + 1, :], act_out[:, f // 2, :, :], ACT.Copy)\
                           .then_inc(hi_done, 1)

            def project_high(c):
                act.wait_ge(proj_done, c + 1)
                for j in range(PER_CHUNK):
                    b, t = PER_CHUNK * c + j, slice(j * SEQ, (j + 1) * SEQ)
                    act.activation(xhi[:, c, t], bank[:, project_bank(c), t], ACT.Identity, bias=emb[:, b:b + 1])\
                       .then_inc(z_hi, 1)

            def round_steps(rnd, last):
                for s in range(STEPS):
                    n = STEPS * rnd + s
                    if s < STEPS - 1:
                        hidden(n + 1, s + 1)
                    elif not last:
                        hidden(n + 1, 0)
                    c = s // EXPERTS - 1
                    if s <= EXPERTS:
                        if s % EXPERTS == 0:
                            tanh_gate(CHUNKS * rnd + CHUNKS - 2 + s // EXPERTS)
                    elif s % EXPERTS == 0 and not last:
                        tanh_gate(CHUNKS * (rnd + 1) + s // EXPERTS - 2)
                    elif s % EXPERTS == 1 and last:
                        project_high(c)
                    if last and s < FFN_PIECES:
                        act.wait_ge(ffn_in[max(0, s - RING + 1)], 16)
                        act.activation(ffn_hi[:, s, :], ffn_raw[:, s % RING, :], ACT.Copy).then_inc(ffn_hi_done, 1)

            def relu_high(b):
                act.wait_ge(cond_h_done, b + 1)
                if b >= 2:
                    act.wait_ge(y_done, b - 1)
                act.activation(hid_hi[:, b % 2, 0:2, :], bank[:, 2 * (b % 2):2 * (b % 2) + 2, :], ACT.Relu)\
                   .then_inc(relu_hi, 1)

            def x0_high(c):
                act.wait_ge(x_in[c], 16)
                act.activation(xhi[:, c, :], x0[:, c, :], ACT.Copy).then_inc(x0_hi, 1)

            def conditioned(c):
                act.wait_ge(y_done, PER_CHUNK * (c + 1))
                if c >= CHUNKS - 2:
                    act.wait_ge(merge_free, 2 * BATCHES)
                act.activation(cur[:, c, :], bank[:, 4 + c % 2, :], ACT.Copy).then_inc(cond_cur, 1)
                act.activation(xhi[:, c, :], bank[:, 4 + c % 2, :], ACT.Copy).then_inc(cond_xhi, 1)

            act.wait_ge(const_done, 1)
            act.activation(low_any[0:1, :], blank[0:1, 0:1], ACT.Gelu_apprx_tanh)
            for m in range(4):
                merged_high(m)
            x0_high(1)
            relu_high(0)
            merged_high(4)
            for b in range(BATCHES):
                c = b // 2 - 1
                if b % 2 == 0 and c >= 0:
                    conditioned(c)
                if 2 * b + 5 < MERGES:
                    merged_high(2 * b + 5)
                if b % 2 == 0 and b >= 2 and c + 2 < CHUNKS:
                    x0_high(c + 2)
                if b + 1 < BATCHES:
                    relu_high(b + 1)
                if 2 * b + 6 < MERGES:
                    merged_high(2 * b + 6)
                for i in MOE_AT.get(b, ()):
                    piece = slice((i % EXPERTS) * F, (i % EXPERTS + 1) * F)
                    act.wait_ge(moe_in[i // 2], 16)
                    act.activation(moe_hi[:, i // EXPERTS, piece], moe_raw[:, i // EXPERTS, piece], ACT.Copy)\
                       .then_inc(moe_hi_done, 1)
                if b % 2 == 1 and c >= 1:
                    tanh_gate(c - 1)

            act.wait_ge(mer_lo_done, 2 * BATCHES)
            hidden(0, 0, True)
            conditioned(CHUNKS - 1)
            with act.Fori(0, ROUNDS - 1) as rnd:
                round_steps(rnd, False)
            round_steps(ROUNDS - 1, True)

            def high(t, pr, done, count):
                if pr == 0 and t < 2:
                    act.wait_ge(y_done, Y_MOE - 1 + t)
                act.wait_ge(done, count)
                act.activation(l1_hi(t)[:, 2 * pr:2 * pr + 2, :], unsplit(t)[:, 2 * pr:2 * pr + 2, :],
                               ACT.Copy).then_inc(hi_done, 1)

            for kind, c in FFN_STAGES:
                if kind == PROJECT:
                    project_high(c)
                    high(hidden_at(GATED, c - 1), 0, unit_done, FC * (c - 1) + 2)
                    high(hidden_at(GATED, c - 1), 1, unit_done, FC * c)
                elif kind == GATED:
                    t = hidden_at(kind, c)
                    if c == 0:
                        act.wait_ge(ffn_lo_done, FFN_PIECES)
                    for f in range(FC):
                        act.wait_ge(gated_done, FC * c + f + 1)
                        if c >= 1:
                            act.wait_ge(unit_done, FC * (c - 1) + f + 1)
                        act.activation(silu[:, f, :], bank[:, gated_bank(c, f), :], ACT.Silu,
                                       scale=vec[:, V_S1 + f:V_S1 + f + 1]).then_inc(silu_done, 1)
                        if f == 1 and c == 0 or f == 2 and c == CHUNKS - 1:
                            high(t, 0, unit_done, FC * c + 2)
                        elif f == 1 and c == 1:
                            high(t - 1, 1, unit_done, FC * c)
                        elif f == 1 and c == 2:
                            high(t - 1, 0, unit_done, FC * (c - 1) + 2)
                    if c >= 2:
                        done = c if c == CHUNKS - 1 else c - 1
                        high(hidden_at(kind, done), 1, unit_done, FC * done + FC)
                elif kind < W3:
                    t, at, v = hidden_at(kind, c), wide_at(kind, c), V_H1 if kind == H1 else V_H2
                    for o in range(FC):
                        act.wait_ge(o_done, FC * at + o + 1)
                        if o % 2 == 0:
                            act.wait_ge(low_done[o // 2], t)
                        act.activation(act_out[:, o // 2, o % 2, :], bank[:, o + FC * (at % 2), :], ACT.Gelu,
                                       scale=vec[:, v + o:v + o + 1]).then_inc(gelu_done, 1)
                        if o >= 2 and (kind, c) == LAST_STAGE:
                            act.wait_ge(gelu_done, FC * at + o + 1)
                            act.activation(l1_hi(t)[:, o, :], unsplit(t)[:, o, :], ACT.Copy).then_inc(hi_done, 1)
                        elif o % 2 == 1:
                            high(t, o // 2, gelu_done, FC * at + o + 1)

        @block.vector
        def _(dve):
            def x0_low(c):
                dve.wait_ge(x0_hi, c + 1)
                dve.tensor_tensor(xlo[:, c, :], x0[:, c, :], xhi[:, c, :].bitcast(F32), ALU.subtract)\
                   .then_inc(x0_split, 1)

            def merged_sum(m):
                if m >= 2 * BATCHES:
                    half = m - 2 * BATCHES
                    dve.wait_ge(mer_hi_done, m + 1)
                    pick = slice(4 * half, 4 * half + 4)
                    dve.tensor_tensor(lang_lo[:, pick, :].rearrange("p b d -> p (b d)"), bank[:, merge_bank(m), :],
                                      lang_hi[:, pick, :].rearrange("p b d -> p (b d)").bitcast(F32),
                                      ALU.subtract).then_inc(merge_free, 1)
                    return
                b = m // 2
                if m == 0:
                    dve.wait_ge(base_in, 16)
                dve.wait_ge(merge_done, m + 1)
                if m >= 4:
                    dve.wait_ge(mer_lo_done, m - 1 if m >= EARLY else m - 3)
                dve.scalar_tensor_tensor(merged(m), bank[:, merge_bank(m), :], COND_ALPHA, base[:, m % 2, :],
                                         ALU.mult, ALU.add).then_inc(merge_free, 1)

            def gate_order(c, rnd):
                q = CHUNKS * rnd + c
                at = GATE_OPS * q
                shape = [SQ, BLOCKS, EXPERTS, EXPERTS]
                dve.wait_ge(logit_done, q + 1)
                dve.transpose(turned[:].rearrange("p t r -> p (t r)"), bank[0:SQ, GATE, :]).then_inc(gate_step, 1)
                dve.wait_ge(gate_step, at + 1)
                dve.tensor_tensor(logit_lo[:], turned[:, :, EXPERTS:2 * EXPERTS],
                                  gbias[:, bass.ds(EXPERTS * rnd, EXPERTS)].unsqueeze(1)
                                  .to_broadcast([SQ, BLOCKS, EXPERTS]), ALU.add).then_inc(gate_step, 1)
                dve.wait_ge(gate_step, at + 2)
                dve.tensor_tensor(logit[:], turned[:, :, 0:EXPERTS], logit_lo[:], ALU.add).then_inc(gate_step, 1)
                dve.wait_ge(gate_step, at + 3)
                dve.tensor_tensor(beats[:], logit[:].unsqueeze(3).to_broadcast(shape),
                                  logit[:].unsqueeze(2).to_broadcast(shape), ALU.is_ge).then_inc(gate_step, 1)
                dve.tensor_reduce(top[:], logit[:], AX_X, ALU.max).then_inc(gate_step, 1)
                dve.wait_ge(gate_step, at + 4)
                dve.tensor_tensor(beats_up[:].rearrange("p t i j -> p t (i j)"),
                                  beats[:].rearrange("p t i j -> p t (i j)"),
                                  upper[:].rearrange("p i j -> p (i j)").unsqueeze(1)
                                  .to_broadcast([SQ, BLOCKS, EXPERTS * EXPERTS]), ALU.mult).then_inc(gate_step, 1)
                dve.wait_ge(gate_step, at + 5)
                dve.tensor_tensor(below[:], logit[:], top[:].unsqueeze(2).to_broadcast([SQ, BLOCKS, EXPERTS]),
                                  ALU.subtract).then_inc(gate_step, 1)
                dve.wait_ge(gate_step, at + 6)
                dve.tensor_tensor(net[:], beats_up[:], beats_up[:].rearrange("p t i j -> p t j i"),
                                  ALU.subtract).then_inc(gate_step, 1)

            def gate_choice(q):
                at = GATE_OPS * q + GATE_HALF
                dve.wait_ge(gate_step, at)
                dve.tensor_reduce(wins[:], net[:], AX_X, ALU.add).then_inc(gate_step, 1)
                dve.wait_ge(gate_step, at + 1)
                dve.tensor_tensor(chosen[:], wins[:], need[:].unsqueeze(1).to_broadcast([SQ, BLOCKS, EXPERTS]),
                                  ALU.is_ge).then_inc(gate_step, 1)
                dve.wait_ge(gate_step, at + 2)
                dve.tensor_tensor(below_ch[:], below[:], chosen[:], ALU.mult).then_inc(gate_step, 1)
                dve.tensor_scalar(half_chosen[:], chosen[:], 0.5, None, ALU.mult).then_inc(gate_step, 1)
                dve.wait_ge(gate_step, at + 3)
                dve.tensor_reduce(second[:], below_ch[:], AX_X, ALU.add).then_inc(gate_step, 1)
                dve.wait_ge(gate_step, at + 5)
                dve.scalar_tensor_tensor(half_gap[:], second[:].unsqueeze(2).to_broadcast([SQ, BLOCKS, EXPERTS]),
                                         -0.5, below[:], ALU.mult, ALU.add).then_inc(gate_step, 1)

            def gate_weights(q, first=False):
                dve.wait_ge(tanh_done, q + 1)
                dve.scalar_tensor_tensor(cw_tok[:, :, 0:EXPERTS], tanh_gap[:], 1.0, half_chosen[:],
                                         ALU.add, ALU.mult).then_inc(cw_done, 1)
                dve.wait_ge(cw_done, q + 1)
                if not first:
                    dve.wait_ge(cw_stored, 16 * q)
                dve.transpose(cw_row[:], cw_tok[:].rearrange("p t r -> p (t r)")).then_inc(cw_turned, 1)

            def hidden_low(n, s):
                for pr in range(2):
                    dve.wait_ge(hi_done, 2 * n + pr + 1)
                    dve.tensor_tensor(hid_lo[:, s % 2, 2 * pr:2 * pr + 2, :], act_out[:, pr, :, :],
                                      hid_hi[:, s % 2, 2 * pr:2 * pr + 2, :].bitcast(F32), ALU.subtract)\
                       .then_inc(lo_done, 1)

            def mixture_sum(rnd, s):
                n, c, e = STEPS * rnd + s, s // EXPERTS, s % EXPERTS
                if e == 0:
                    dve.wait_ge(cw_ready[c % 2], 16 * (2 * rnd + c // 2 + 1))
                dve.wait_ge(y_done, Y_COND + n + 1)
                dve.wait_ge(add_done, n + 1)
                dve.scalar_tensor_tensor(prod[:, s % 2, :], bank[:, 4 + s % 2, :], vec[:, V_B2 + e:V_B2 + e + 1],
                                         cw_all[:, c % 2, e, :], ALU.add, ALU.mult).then_inc(prod_done, 1)
                if e == EXPERTS - 1:
                    dve.wait_ge(prod_done, n + 1)
                    dve.wait_ge(add_done, ADD0 + n)
                    dve.tensor_tensor(cur[:, c, :], cur[:, c, :], prod[:, s % 2, :], ALU.add).then_inc(add_done, 1)

            def round_steps(rnd, last):
                for s in range(STEPS):
                    n, c, e = STEPS * rnd + s, s // EXPERTS, s % EXPERTS
                    if s <= EXPERTS + 1:
                        if e == 1:
                            gate_weights(CHUNKS * rnd + CHUNKS - 2 + c)
                    elif e == 1 and not last:
                        gate_weights(CHUNKS * (rnd + 1) + c - 2)
                    if s < STEPS - 1:
                        hidden_low(n + 1, s + 1)
                    elif not last:
                        hidden_low(n + 1, 0)
                    if last and e == 1 and c >= 1:
                        project_low(c - 1)
                    if last and s == STEPS - 1:
                        return
                    mixture_sum(rnd, s)
                    if s == 1:
                        gate_order(CHUNKS - 1, rnd)
                    elif s == 2:
                        gate_choice(CHUNKS * rnd + CHUNKS - 1)
                        if not last:
                            dve.tensor_copy(wg_now[:], wg[:, bass.ds(rnd + 1, 1), :].rearrange("p r e -> p (r e)"))\
                               .then_inc(wg_done, 1)
                    elif e == 1 and not last:
                        gate_order(c - 1, rnd + 1)
                    elif e == 2 and not last:
                        gate_choice(CHUNKS * (rnd + 1) + c - 1)
                    if last and 1 <= s <= FFN_PIECES:
                        dve.wait_ge(ffn_lo_done, s)
                        dve.tensor_reduce(low_max[:, s - 1:s], ffn_lo[:, s - 1, :].bitcast(F32), AX_X, ALU.max,
                                          apply_absolute_value=True).then_inc(low_max_done, 1)
                    elif last and s == FFN_PIECES + 1:
                        dve.wait_ge(low_max_done, FFN_PIECES)
                        dve.tensor_reduce(low_row[:], low_max[:], AX_X, ALU.max).then_inc(low_max_done, 1)
                    if e == EXPERTS - 1:
                        split_cur(rnd, c)

            def cur_high(rnd, c):
                dve.wait_ge(add_done, ADD0 + STEPS * rnd + EXPERTS * c + EXPERTS)
                dve.tensor_copy(xhi[:, c, :], cur[:, c, :]).then_inc(xhi_done, 1)

            def split_cur(rnd, c):
                cur_high(rnd, c)
                dve.wait_ge(xhi_done, CHUNKS * rnd + c + 1)
                dve.tensor_tensor(xlo[:, c, :], cur[:, c, :], xhi[:, c, :].bitcast(F32), ALU.subtract)\
                   .then_inc(xs_done, 1)

            def project_low(c):
                dve.wait_ge(z_hi, PER_CHUNK * c + PER_CHUNK)
                for j in range(PER_CHUNK):
                    b, t = PER_CHUNK * c + j, slice(j * SEQ, (j + 1) * SEQ)
                    dve.scalar_tensor_tensor(xlo[:, c, t], bank[:, project_bank(c), t], emb[:, b:b + 1],
                                             xhi[:, c, t].bitcast(F32), ALU.add, ALU.subtract).then_inc(evac_done, 1)

            def split_gate():
                dve.wait_ge(const_done, 2)
                dve.wait_ge(small_in, 32)
                dve.tensor_copy(wg_raw[:, :, 0:EXPERTS], vec[:, V_WG:V_N].rearrange("p (r e) -> p r e", e=EXPERTS))\
                   .then_inc(wg_step, 1)
                dve.wait_ge(wg_step, 1)
                dve.tensor_copy(wg[:], wg_raw[:]).then_inc(wg_step, 1)
                dve.wait_ge(wg_step, 2)
                dve.tensor_tensor(wg[:, :, EXPERTS:2 * EXPERTS], wg_raw[:, :, 0:EXPERTS],
                                  wg[:, :, 0:EXPERTS].bitcast(F32), ALU.subtract).then_inc(wg_step, 1)
                dve.wait_ge(wg_step, 3)
                dve.tensor_copy(wg_now[:], wg[:, 0, :]).then_inc(wg_done, 1)

            def relu_low(b):
                dve.wait_ge(relu_hi, b + 1)
                dve.scalar_tensor_tensor(hid_lo[:, b % 2, 0:2, :], bank[:, 2 * (b % 2):2 * (b % 2) + 2, :], 0.0,
                                         hid_hi[:, b % 2, 0:2, :].bitcast(F32), ALU.max, ALU.subtract)\
                   .then_inc(relu_lo, 1)

            for m in range(4):
                merged_sum(m)
                if m == 1:
                    dve.wait_ge(x_in[0], 16)
                    dve.tensor_copy(xhi[:, 0, :], x0[:, 0, :]).then_inc(x0_hi, 1)
                    x0_low(0)
            x0_low(1)
            merged_sum(4)
            relu_low(0)
            for b in range(BATCHES):
                c = b // 2 - 1
                if 2 * b + 5 < MERGES:
                    merged_sum(2 * b + 5)
                if b % 2 == 0 and c >= 0:
                    if c + 2 < CHUNKS:
                        x0_low(c + 2)
                elif c >= 0:
                    if c == 0:
                        dve.wait_ge(const_done, CONSTS)
                    gate_order(c, 0)
                if 2 * b + 6 < MERGES:
                    merged_sum(2 * b + 6)
                if b + 1 < BATCHES:
                    relu_low(b + 1)
                if b == 1:
                    split_gate()
                if b % 2 == 0 and c >= 1:
                    gate_choice(c - 1)
                elif c >= 1:
                    gate_weights(c - 1, c == 1)
            hidden_low(0, 0)
            gate_choice(CHUNKS - 2)
            with dve.Fori(0, ROUNDS - 1) as rnd:
                round_steps(rnd, False)
            round_steps(ROUNDS - 1, True)

            def stage_low(t, pr):
                dve.wait_ge(hi_done, LO_MOE + 2 * t + pr + 1)
                dve.tensor_tensor(l1_lo(t)[:, 2 * pr:2 * pr + 2, :], unsplit(t)[:, 2 * pr:2 * pr + 2, :],
                                  l1_hi(t)[:, 2 * pr:2 * pr + 2, :].bitcast(F32), ALU.subtract)\
                   .then_inc(low_done[pr], 1)

            for kind, c in FFN_STAGES:
                if kind == PROJECT:
                    project_low(c)
                    stage_low(hidden_at(GATED, c - 1), 1)
                elif kind == W3:
                    dve.wait_ge(y_done, Y_MOE + c + 1)
                    for t in out_parts(c):
                        dve.scalar_tensor_tensor(x0[:, c, t], bank[:, out_bank(c), t], vec[:, V_S3:V_S3 + 1],
                                                 cur[:, c, t], ALU.mult, ALU.add).then_inc(evac_done, 1)
                else:
                    t = hidden_at(kind, c)
                    if kind == GATED:
                        for f in range(FC):
                            if f == 2 and c == 1:
                                stage_low(t - 1, 1)
                            dve.wait_ge(silu_done, FC * c + f + 1)
                            if c >= 2 and f % 2 == 0:
                                dve.wait_ge(low_done[f // 2], t - 1)
                            dve.scalar_tensor_tensor(unsplit(t)[:, f, :], bank[:, gated_bank(c, f) + 1, :],
                                                     vec[:, V_S2 + f:V_S2 + f + 1], silu[:, f, :],
                                                     ALU.mult, ALU.mult).then_inc(unit_done, 1)
                            if c == 0 and f == 1:
                                mixture_sum(ROUNDS - 1, STEPS - 1)
                        if c == 0:
                            cur_high(ROUNDS - 1, CHUNKS - 1)
                        elif c >= 2:
                            stage_low(t if c == CHUNKS - 1 else t - 1, 1)
                    elif (kind, c) == LAST_STAGE:
                        stage_low(t, 0)
                        for o in range(2, FC):
                            dve.wait_ge(hi_done, LO_MOE + 2 * t + o)
                            dve.tensor_tensor(l1_lo(t)[:, o, :], unsplit(t)[:, o, :], l1_hi(t)[:, o, :].bitcast(F32),
                                              ALU.subtract).then_inc(low_done[1], 1)
                    else:
                        for pr in range(2):
                            stage_low(t, pr)


def kernel(**inputs):
    import numpy as np
    import concourse.bacc as bacc
    from concourse.bass_utils import run_bass_kernel_spmd

    a = {k: np.asarray(v) for k, v in inputs.items()}

    def down(w):
        return w.T.reshape(-1, P, w.shape[0]).transpose(1, 0, 2)

    def cols(v):
        return v.reshape(-1, P).T

    def factors(ia, ib, oa, ob):
        return np.concatenate([ia, np.swapaxes(ib, -1, -2), oa, np.swapaxes(ob, -1, -2)], axis=-1)

    c, f, g = "L0_cond_", "L0_ffn_", "L1_ffn_"
    common, expert = (factors(*(a[f"{c}{kind}_{w}"] for w in ("wi_a", "wi_b", "wo_a", "wo_b")))
                      for kind in ("common", "experts"))
    arrays = {
        "x_t": a["x"].reshape(TOKENS, D).T,
        "batch_ids": np.concatenate([a["itok_B_0_7"], a["itok_B_0_3"]]).reshape(1, 2 * BATCHES),
        "cond_base": np.stack([a[c + "wi"].T, down(a[c + "wo"]).reshape(P, F)], axis=1),
        "lora_all": np.concatenate([np.broadcast_to(common, expert.shape), expert], axis=1),
        "lang_lora": np.concatenate([a["L1_cond_lora_A"], np.swapaxes(a["L1_cond_lora_B"], 1, 2)], axis=2),
        "lang_embed": a["L1_cond_lang_embed"],
        "moe_w": np.stack([a[f + "W1"].transpose(1, 0, 2).reshape(P, EXPERTS * F),
                           a[f + "W2"].reshape(EXPERTS * FC, P, D).transpose(1, 0, 2).reshape(P, EXPERTS * F)], axis=1),
        "vecs": np.concatenate([cols(a[f + "b1"]), cols(a[f + "b2"]), cols(a[g + "w1_s"]), cols(a[g + "w2_s"]),
                                cols(a[g + "h1_s"]), cols(a[g + "h2_s"]), cols(a[g + "w3_s"]),
                                a[f + "Wg"].transpose(1, 0, 2).reshape(P, ROUNDS * EXPERTS)], axis=1),
        "gate_bias": a[f + "bg"].reshape(1, ROUNDS * EXPERTS),
        "ffn_w": np.concatenate([a[g + "w1_w"].T[:, None, :], a[g + "w2_w"].T[:, None, :], down(a[g + "h1_w"]),
                                 down(a[g + "h2_w"]), down(a[g + "w3_w"]).reshape(P, 1, F)], axis=1),
    }
    arrays = {k: np.ascontiguousarray(v) for k, v in arrays.items()}
    nc = bacc.Bacc("TRN2", target_bir_lowering=False, num_devices=1)
    args = [nc.dram_tensor(k, v.shape, mybir.dt.from_np(v.dtype), kind="ExternalInput").ap()
            for k, v in arrays.items()]
    out = nc.dram_tensor("out_t", (P, TOKENS), F32, kind="ExternalOutput").ap()
    adaln_ffn(nc, *args, out)
    r = run_bass_kernel_spmd(nc, [arrays], core_ids=[0])
    return np.ascontiguousarray(r.results[0]["out_t"].T).reshape(BATCHES, SEQ, D)
```
